# Optimizing a Trainium2 kernel written in Bass

```python
import numpy as np
import jax
import jax.numpy as jnp

def _softmax(x, axis=-1):
    return jax.nn.softmax(x, axis=axis)

def _gelu(x):
    return jax.nn.gelu(x, approximate=True)

def _silu(x):
    return jax.nn.silu(x)

def _sigmoid(x):
    return jax.nn.sigmoid(x)

def _layernorm(x, axis=-1, eps=1e-05):
    m = jnp.mean(x, axis=axis, keepdims=True)
    v = jnp.var(x, axis=axis, keepdims=True)
    return (x - m) / jnp.sqrt(v + eps)

def _scatter_add(tgt, idx, src, axis=0):
    return tgt.at[idx].add(src)

def _segment_sum(src, seg, n):
    return jax.ops.segment_sum(src, seg, n)
kernel_name = 'mk_xattn_seq_d4_seqx_r8_5d1ffe'

def setup_inputs(seed: int=0):
    np.random.seed(seed)
    _w = jnp.asarray

    def _rec_inputs():
        import jax
        import jax.numpy as jnp
        _rk = jax.random.key(seed)
        x = -0.0002928 + 1 * jax.random.normal(jax.random.fold_in(_rk, 1), (64, 64, 256), jnp.float32)
        _lenS = 64 - jax.random.randint(jax.random.fold_in(_rk, 7), (64,), 0, max(1, 64 // 4) + 1, jnp.int32)
        _lenS2 = 64 - jax.random.randint(jax.random.fold_in(_rk, 8), (64,), 0, max(1, 64 // 4) + 1, jnp.int32)
        _ctx_2048P = jax.random.normal(jax.random.fold_in(_rk, 11), (64, 16, 256), jnp.float32)
        _ctx_2048c = jax.random.dirichlet(jax.random.fold_in(_rk, 511), 0.3 * jnp.ones((16,), jnp.float32), (64, 64))
        _ctx_2048t = jnp.einsum('bsk,bkd->bsd', _ctx_2048c, _ctx_2048P)
        _ctx_2048t = _ctx_2048t * jax.lax.rsqrt(jnp.mean(jnp.square(_ctx_2048t)) + 1e-12) * 0.953939
        ctx_2048 = -1.39393e-06 + 0.999914 * (_ctx_2048t + 0.3 * jax.random.normal(jax.random.fold_in(_rk, 611), (64, 64, 256), jnp.float32))
        _validS = jnp.arange(64)[None, :] < _lenS[:, None]
        _validS2 = jnp.arange(64)[None, :] < _lenS2[:, None]
        _causal = jnp.tril(jnp.ones((64, 64), dtype=bool))
        mask_BxS2_bf1 = jnp.ones((64, 64), dtype=bool)
        return (x, ctx_2048, mask_BxS2_bf1)
    x, ctx_2048, mask_BxS2_bf1 = _rec_inputs()

    def _L0_xattn_setup():
        import jax, jax.numpy as jnp
        import numpy as np
        EPS = 1e-05

        def _inorm(x):
            m = jnp.mean(x, axis=-1, keepdims=True)
            v = jnp.var(x, axis=-1, keepdims=True)
            return (x - m) * jax.lax.rsqrt(v + EPS)

        def _conv1x1(W, b, x):
            return jnp.einsum('oc,bct->bot', W, x) + b[None, :, None]
        key = jax.random.key(seed)
        ks = jax.random.split(key, 10)
        B, C, T = (4, 64, 256)
        s = 1.0 / np.sqrt(C)
        return {'x_c': jax.random.normal(ks[0], (B, C, T), jnp.float32), 'x_s': jax.random.normal(ks[1], (B, C, T), jnp.float32), 'Wn': jax.random.normal(ks[2], (C, C), jnp.float32) * s, 'bn': jax.random.normal(ks[3], (C,), jnp.float32) * s, 'Wm': jax.random.normal(ks[4], (C, C), jnp.float32) * s, 'bm': jax.random.normal(ks[5], (C,), jnp.float32) * s, 'Wl': jax.random.normal(ks[6], (C, C), jnp.float32) * s, 'bl': jax.random.normal(ks[7], (C,), jnp.float32) * s, 'Wo': jax.random.normal(ks[8], (C, C), jnp.float32) * s, 'bo': jax.random.normal(ks[9], (C,), jnp.float32) * s}
    _L0_xattn_all = _L0_xattn_setup()
    _L0_xattn_in = {k: v for k, v in _L0_xattn_all.items() if k in ('Wn', 'bn', 'Wm', 'bm', 'Wl', 'bl', 'Wo', 'bo')}
    del _L0_xattn_all

    def _L1_xattn_setup():
        import jax, jax.numpy as jnp
        import numpy as np
        HIDDEN = 256
        HEADS = 16
        HEAD_DIM = HIDDEN // HEADS
        LN_EPS = 1e-05
        GATE_INIT = 0.5

        def _layer_norm(x, gamma, beta):
            mu = jnp.mean(x, axis=-1, keepdims=True)
            var = jnp.mean(jnp.square(x - mu), axis=-1, keepdims=True)
            return (x - mu) * jax.lax.rsqrt(var + LN_EPS) * gamma + beta
        key = jax.random.key(seed)
        ks = jax.random.split(key, 8)
        B, T_TEXT, T_AUDIO = (4, 256, 1500)
        s = 0.02
        return {'hidden_states': jax.random.normal(ks[0], (B, T_TEXT, HIDDEN), jnp.float32), 'audio_kv': jax.random.normal(ks[1], (B, T_AUDIO, HIDDEN), jnp.float32), 'audio_attention_mask': jnp.ones((B, T_AUDIO), dtype=bool), 'Wq': jax.random.normal(ks[2], (HIDDEN, HIDDEN), jnp.float32) * s, 'Wk': jax.random.normal(ks[3], (HIDDEN, HIDDEN), jnp.float32) * s, 'Wv': jax.random.normal(ks[4], (HIDDEN, HIDDEN), jnp.float32) * s, 'Wo': jax.random.normal(ks[5], (HIDDEN, HIDDEN), jnp.float32) * s, 'ln_gamma': jnp.ones((HIDDEN,), jnp.float32), 'ln_beta': jnp.zeros((HIDDEN,), jnp.float32), 'gate': jnp.array([GATE_INIT], jnp.float32)}
    _L1_xattn_all = _L1_xattn_setup()
    _L1_xattn_in = {k: v for k, v in _L1_xattn_all.items() if k in ('Wq', 'Wk', 'Wv', 'Wo', 'ln_gamma', 'ln_beta', 'gate')}
    del _L1_xattn_all

    def _L2_xattn_setup():
        import jax, jax.numpy as jnp
        import numpy as np
        HIDDEN = 256
        HEADS = 16
        HEAD_DIM = HIDDEN // HEADS
        LN_EPS = 1e-05
        GATE_INIT = 0.5

        def _layer_norm(x, gamma, beta):
            mu = jnp.mean(x, axis=-1, keepdims=True)
            var = jnp.mean(jnp.square(x - mu), axis=-1, keepdims=True)
            return (x - mu) * jax.lax.rsqrt(var + LN_EPS) * gamma + beta
        key = jax.random.key(seed)
        ks = jax.random.split(key, 8)
        B, T_TEXT, T_AUDIO = (4, 256, 1500)
        s = 0.02
        return {'hidden_states': jax.random.normal(ks[0], (B, T_TEXT, HIDDEN), jnp.float32), 'audio_kv': jax.random.normal(ks[1], (B, T_AUDIO, HIDDEN), jnp.float32), 'audio_attention_mask': jnp.ones((B, T_AUDIO), dtype=bool), 'Wq': jax.random.normal(ks[2], (HIDDEN, HIDDEN), jnp.float32) * s, 'Wk': jax.random.normal(ks[3], (HIDDEN, HIDDEN), jnp.float32) * s, 'Wv': jax.random.normal(ks[4], (HIDDEN, HIDDEN), jnp.float32) * s, 'Wo': jax.random.normal(ks[5], (HIDDEN, HIDDEN), jnp.float32) * s, 'ln_gamma': jnp.ones((HIDDEN,), jnp.float32), 'ln_beta': jnp.zeros((HIDDEN,), jnp.float32), 'gate': jnp.array([GATE_INIT], jnp.float32)}
    _L2_xattn_all = _L2_xattn_setup()
    _L2_xattn_in = {k: v for k, v in _L2_xattn_all.items() if k in ('Wq', 'Wk', 'Wv', 'Wo', 'ln_gamma', 'ln_beta', 'gate')}
    del _L2_xattn_all

    def _L3_xattn_setup():
        import jax, jax.numpy as jnp
        import numpy as np
        H = 256
        B, L, S = (4, 512, 10)
        key = jax.random.key(seed)
        k1, k2, k3, k4, k5, k6 = jax.random.split(key, 6)
        scale = 1.0 / np.sqrt(H)
        return {'h_english': jax.random.normal(k1, (B, L, H), dtype=jnp.float32), 'h_lojban': jax.random.normal(k2, (B, S, H), dtype=jnp.float32), 'w_q': jax.random.normal(k3, (H, H), dtype=jnp.float32) * scale, 'w_k': jax.random.normal(k4, (H, H), dtype=jnp.float32) * scale, 'w_v': jax.random.normal(k5, (H, H), dtype=jnp.float32) * scale, 'w_o': jax.random.normal(k6, (H, H), dtype=jnp.float32) * scale, 'alpha': jnp.float32(0.1)}
    _L3_xattn_all = _L3_xattn_setup()
    _L3_xattn_in = {k: v for k, v in _L3_xattn_all.items() if k in ('w_q', 'w_k', 'w_v', 'w_o', 'alpha')}
    del _L3_xattn_all
    return {'x': x, 'ctx_2048': ctx_2048, 'mask_BxS2_bf1': mask_BxS2_bf1, 'L0_xattn_Wn': _L0_xattn_in['Wn'], 'L0_xattn_bn': _L0_xattn_in['bn'], 'L0_xattn_Wm': _L0_xattn_in['Wm'], 'L0_xattn_bm': _L0_xattn_in['bm'], 'L0_xattn_Wl': _L0_xattn_in['Wl'], 'L0_xattn_bl': _L0_xattn_in['bl'], 'L0_xattn_Wo': _L0_xattn_in['Wo'], 'L0_xattn_bo': _L0_xattn_in['bo'], 'L1_xattn_Wq': _L1_xattn_in['Wq'], 'L1_xattn_Wk': _L1_xattn_in['Wk'], 'L1_xattn_Wv': _L1_xattn_in['Wv'], 'L1_xattn_Wo': _L1_xattn_in['Wo'], 'L1_xattn_ln_gamma': _L1_xattn_in['ln_gamma'], 'L1_xattn_ln_beta': _L1_xattn_in['ln_beta'], 'L1_xattn_gate': _L1_xattn_in['gate'], 'L2_xattn_Wq': _L2_xattn_in['Wq'], 'L2_xattn_Wk': _L2_xattn_in['Wk'], 'L2_xattn_Wv': _L2_xattn_in['Wv'], 'L2_xattn_Wo': _L2_xattn_in['Wo'], 'L2_xattn_ln_gamma': _L2_xattn_in['ln_gamma'], 'L2_xattn_ln_beta': _L2_xattn_in['ln_beta'], 'L2_xattn_gate': _L2_xattn_in['gate'], 'L3_xattn_w_q': _L3_xattn_in['w_q'], 'L3_xattn_w_k': _L3_xattn_in['w_k'], 'L3_xattn_w_v': _L3_xattn_in['w_v'], 'L3_xattn_w_o': _L3_xattn_in['w_o'], 'L3_xattn_alpha': _L3_xattn_in['alpha']}

def reference(x, ctx_2048, mask_BxS2_bf1, L0_xattn_Wn, L0_xattn_bn, L0_xattn_Wm, L0_xattn_bm, L0_xattn_Wl, L0_xattn_bl, L0_xattn_Wo, L0_xattn_bo, L1_xattn_Wq, L1_xattn_Wk, L1_xattn_Wv, L1_xattn_Wo, L1_xattn_ln_gamma, L1_xattn_ln_beta, L1_xattn_gate, L2_xattn_Wq, L2_xattn_Wk, L2_xattn_Wv, L2_xattn_Wo, L2_xattn_ln_gamma, L2_xattn_ln_beta, L2_xattn_gate, L3_xattn_w_q, L3_xattn_w_k, L3_xattn_w_v, L3_xattn_w_o, L3_xattn_alpha):
    import jax
    import jax.numpy as jnp

    def _L0_xattn_ref(x_c, x_s, Wn, bn, Wm, bm, Wl, bl, Wo, bo):
        import jax, jax.numpy as jnp
        import numpy as np
        EPS = 1e-05

        def _inorm(x):
            m = jnp.mean(x, axis=-1, keepdims=True)
            v = jnp.var(x, axis=-1, keepdims=True)
            return (x - m) * jax.lax.rsqrt(v + EPS)

        def _conv1x1(W, b, x):
            return jnp.einsum('oc,bct->bot', W, x) + b[None, :, None]
        Mn = _conv1x1(Wn, bn, _inorm(x_c))
        Mm = _conv1x1(Wm, bm, _inorm(x_s))
        A = jax.nn.softmax(jnp.einsum('bct,bcs->bts', Mn, Mm), axis=-1)
        Ml = _conv1x1(Wl, bl, x_s)
        Mo = jnp.einsum('bcs,bts->bct', Ml, A)
        return _conv1x1(Wo, bo, Mo) + x_c

    def _L1_xattn_ref(hidden_states, audio_kv, audio_attention_mask, Wq, Wk, Wv, Wo, ln_gamma, ln_beta, gate):
        import jax, jax.numpy as jnp
        import numpy as np
        HIDDEN = 256
        HEADS = 16
        HEAD_DIM = HIDDEN // HEADS
        LN_EPS = 1e-05
        GATE_INIT = 0.5

        def _layer_norm(x, gamma, beta):
            mu = jnp.mean(x, axis=-1, keepdims=True)
            var = jnp.mean(jnp.square(x - mu), axis=-1, keepdims=True)
            return (x - mu) * jax.lax.rsqrt(var + LN_EPS) * gamma + beta
        B, Tt, D = hidden_states.shape
        Ta = audio_kv.shape[1]
        scale = HEAD_DIM ** (-0.5)
        a = _layer_norm(audio_kv, ln_gamma, ln_beta)
        Q = (hidden_states @ Wq.T).reshape(B, Tt, HEADS, HEAD_DIM).transpose(0, 2, 1, 3)
        K = (a @ Wk.T).reshape(B, Ta, HEADS, HEAD_DIM).transpose(0, 2, 1, 3)
        V = (a @ Wv.T).reshape(B, Ta, HEADS, HEAD_DIM).transpose(0, 2, 1, 3)
        scores = jnp.einsum('bhtd,bhsd->bhts', Q, K) * scale
        mask = audio_attention_mask[:, None, None, :]
        scores = jnp.where(mask, scores, jnp.float32(-jnp.inf))
        attn = jax.nn.softmax(scores, axis=-1)
        out = jnp.einsum('bhts,bhsd->bhtd', attn, V)
        out = out.transpose(0, 2, 1, 3).reshape(B, Tt, D)
        out = out @ Wo.T
        return hidden_states + jnp.tanh(gate) * out

    def _L2_xattn_ref(hidden_states, audio_kv, audio_attention_mask, Wq, Wk, Wv, Wo, ln_gamma, ln_beta, gate):
        import jax, jax.numpy as jnp
        import numpy as np
        HIDDEN = 256
        HEADS = 16
        HEAD_DIM = HIDDEN // HEADS
        LN_EPS = 1e-05
        GATE_INIT = 0.5

        def _layer_norm(x, gamma, beta):
            mu = jnp.mean(x, axis=-1, keepdims=True)
            var = jnp.mean(jnp.square(x - mu), axis=-1, keepdims=True)
            return (x - mu) * jax.lax.rsqrt(var + LN_EPS) * gamma + beta
        B, Tt, D = hidden_states.shape
        Ta = audio_kv.shape[1]
        scale = HEAD_DIM ** (-0.5)
        a = _layer_norm(audio_kv, ln_gamma, ln_beta)
        Q = (hidden_states @ Wq.T).reshape(B, Tt, HEADS, HEAD_DIM).transpose(0, 2, 1, 3)
        K = (a @ Wk.T).reshape(B, Ta, HEADS, HEAD_DIM).transpose(0, 2, 1, 3)
        V = (a @ Wv.T).reshape(B, Ta, HEADS, HEAD_DIM).transpose(0, 2, 1, 3)
        scores = jnp.einsum('bhtd,bhsd->bhts', Q, K) * scale
        mask = audio_attention_mask[:, None, None, :]
        scores = jnp.where(mask, scores, jnp.float32(-jnp.inf))
        attn = jax.nn.softmax(scores, axis=-1)
        out = jnp.einsum('bhts,bhsd->bhtd', attn, V)
        out = out.transpose(0, 2, 1, 3).reshape(B, Tt, D)
        out = out @ Wo.T
        return hidden_states + jnp.tanh(gate) * out

    def _L3_xattn_ref(h_english, h_lojban, w_q, w_k, w_v, w_o, alpha):
        import jax, jax.numpy as jnp
        import numpy as np
        H = 256
        B, L, S = (4, 512, 10)
        h = h_english.shape[-1]
        q = jnp.einsum('blh,oh->blo', h_english, w_q)
        k = jnp.einsum('bsh,oh->bso', h_lojban, w_k)
        v = jnp.einsum('bsh,oh->bso', h_lojban, w_v)
        scores = jnp.einsum('blh,bsh->bls', q, k) / jnp.sqrt(jnp.float32(h))
        probs = jax.nn.softmax(scores, axis=-1)
        context = jnp.einsum('bls,bsh->blh', probs, v)
        delta = jnp.einsum('blh,oh->blo', context, w_o)
        return h_english + alpha * delta
    x = _L0_xattn_ref(x, ctx_2048, L0_xattn_Wn, L0_xattn_bn, L0_xattn_Wm, L0_xattn_bm, L0_xattn_Wl, L0_xattn_bl, L0_xattn_Wo, L0_xattn_bo)
    x = _L1_xattn_ref(x, ctx_2048, mask_BxS2_bf1, L1_xattn_Wq, L1_xattn_Wk, L1_xattn_Wv, L1_xattn_Wo, L1_xattn_ln_gamma, L1_xattn_ln_beta, L1_xattn_gate)
    x = _L2_xattn_ref(x, ctx_2048, mask_BxS2_bf1, L2_xattn_Wq, L2_xattn_Wk, L2_xattn_Wv, L2_xattn_Wo, L2_xattn_ln_gamma, L2_xattn_ln_beta, L2_xattn_gate)
    x = _L3_xattn_ref(x, ctx_2048, L3_xattn_w_q, L3_xattn_w_k, L3_xattn_w_v, L3_xattn_w_o, L3_xattn_alpha)
    return x

_drawn_inputs = setup_inputs


def setup_inputs(seed=0):
    import zlib

    import numpy as np

    out = dict(_drawn_inputs(seed))
    spreads = {'L1_xattn_ln_gamma': (1.0, 0.6),
     'L1_xattn_ln_beta': (0.0, 0.8),
     'L2_xattn_ln_gamma': (1.0, 0.6),
     'L2_xattn_ln_beta': (0.0, 0.8)}
    factors = {'L0_xattn_bm': 8.0,
     'L1_xattn_Wq': 8.0,
     'L1_xattn_Wk': 8.0,
     'L1_xattn_Wv': 3.338,
     'L1_xattn_Wo': 3.384,
     'L2_xattn_Wq': 8.0,
     'L2_xattn_Wk': 8.0,
     'L2_xattn_Wv': 3.386,
     'L2_xattn_Wo': 3.42}
    for name, (base, spread) in spreads.items():
        noise = np.random.default_rng([zlib.crc32(name.encode()), seed]).standard_normal(out[name].shape)
        drawn = base * np.exp(spread * noise) if base else spread * noise
        out[name] = jnp.asarray(drawn.astype(out[name].dtype))
    for name, factor in factors.items():
        out[name] = (out[name] * factor).astype(out[name].dtype)
    return out
```

```python
from contextlib import ExitStack

import concourse.bass as bass
from concourse import mybir

F32 = mybir.dt.float32
F32R = mybir.dt.float32r
U8 = mybir.dt.uint8
ALU = mybir.AluOpType
ACT = mybir.ActivationFunctionType
AX_X = mybir.AxisListType.X

P = 128
B, C, D = 64, 64, 256
NH, HD = 16, 16
GB = 8
NG = B // GB
NP = GB // 2
TOK = GB * C
NK = D // P
NJ = NH // 2
EPS = 1e-5
VW = HD * 2 + 1
V0W = C + 1


def group_order(front):
    o = [("S", 0, 0), ("S", 0, 1), ("X", 0, 0), ("P", "K1", 0), ("T", 0, 0)]
    for b in range(2, GB):
        o += [("S", 0, b), ("X", 0, b - 1), ("A", 0, b - 2), ("T", 0, b - 1)]
    o += [("X", 0, GB - 1), ("P", "V1", 0), ("A", 0, GB - 2), ("T", 0, GB - 1), ("P", "V1", 1), ("A", 0, GB - 1),
          ("P", "K1", 1)]
    for l in (1, 2):
        k, v = f"K{l + 1}", f"V{l + 1}"
        o += [("P", f"Q{l}", 0), ("P", f"Q{l}", 1), ("S", l, 0), ("S", l, 1), ("P", v, 0), ("X", l, 0)]
        if front and l == 2:
            o += [("MG", 0)]
        o += [("S", l, 2), ("X", l, 1), ("S", l, 3)]
        for p in range(3):
            o += [("T", l, p), ("X", l, 2 * p + 2), ("S", l, 2 * p + 4)] if p < 2 else [("T", l, p)]
            if front and l == 1 and p < 2:
                o += [("ST", 2 * p)]
            if p < 2:
                o += [("A", l, p), ("X", l, 2 * p + 3), ("S", l, 2 * p + 5)]
            if front and l == 1 and p < 2:
                o += [("ST", 2 * p + 1)]
        o += [("X", l, 6), ("P", v, 1), ("A", l, 2), ("X", l, 7), ("T", l, 3), ("P", f"AT{l}", 0), ("P", k, 0), ("A", l, 3),
              ("P", k, 1), ("P", f"AT{l}", 1), ("P", f"O{l}", 0), ("P", f"O{l}", 1)]
    if front:
        o += front_order()[:4]
    o += [("S", 3, 0), ("S", 3, 1)]
    if front:
        o += front_order()[4:6]
    o += [("X", 3, 0), ("X", 3, 1), ("T", 3, 0), ("P", "XN", 0), ("T", 3, 1), ("P", "XN", 1)]
    if front:
        o += front_order()[6:8]
    o += [("P", "PV", 0), ("P", "PV", 1)]
    if front:
        o += front_order()[8:]
    return o


def front_order():
    return [("P", n, i) for n in ("xT", "cT", "aT", "Mn", "Mm", "V0") for i in range(2)]


WEIGHT_STEPS = [("P", n, 0) for n in ("W0T", "W0", "MS", "Wo3T", "M3", "VW3")] + \
    [("P", f"W{n}{l}", 0) for l in (1, 2) for n in "qkvo"]


def build(nc, x, ctx_in, mask, w, cst_ident, cst_block, cst_parity, out):
    ORDER = group_order(True)
    LAST_ORDER = group_order(False)
    PROLOGUE = WEIGHT_STEPS + front_order()

    def numbered(order, kind):
        n, at = 0, {}
        for s in order:
            if kind == "A" and s[0] == "A" and s[1] == 0:
                at[s] = n
                n += s[2] % 2
            elif s[0] == kind:
                per = {"T": {1: 2, 2: 2}, "A": {1: 2, 2: 2}}.get(kind, {}).get(s[1], 1)
                at[s] = n
                n += per
        return at, n

    p_at, p_n = numbered(ORDER, "P")
    p_at_last, _ = numbered(LAST_ORDER, "P")
    p_at_pro, p_n_pro = numbered(PROLOGUE, "P")
    s_at, s_n = numbered(ORDER, "S")
    t_at, t_n = numbered(ORDER, "T")
    a_at, a_n = numbered(ORDER, "A")
    assert p_n % 2 == 0 and p_n_pro % 2 == 0 and s_n % 2 == 0 and t_n % 2 == 0 and a_n % 2 == 0
    P_BASE = p_n_pro // 2

    def p_count(g, step, last):
        if g is None:
            n = p_at_pro[step]
            return n % 2, n // 2 + 1
        n = (p_at_last if last else p_at)[step]
        return n % 2, g * (p_n // 2) + (P_BASE + n // 2 + 1)

    def ring_count(g, n, total):
        fills = g * (total // 2) + (n // 2 + 1)
        return n % 2, fills, g * (total // 2) + (n // 2 + 2)

    with ExitStack() as stack:
        def sb(name, shape, dt=F32):
            return stack.enter_context(nc.sbuf_tensor(name, shape, dt))

        def pair_of(name, shape):
            return sb(name + "_hi", shape, F32R), sb(name + "_lo", shape, F32R)

        def sem(name):
            return stack.enter_context(nc.semaphore(name))

        def bank(name):
            return stack.enter_context(nc.psum_tensor(name, [P, 512], F32))

        ident = sb("ident", [P, P])
        block = sb("block", [P, P])
        parity = sb("parity", [P, 2])
        w0_bd = sb("w0_bd", [P, 4, P])
        w0_cols = sb("w0_cols", [P, 3])
        bo_row = sb("bo_row", [P, 2, C])
        w0T = sb("w0T", [P, 3, P])
        bl_wide = sb("bl_wide", [P, P])
        wv0 = sb("wv0", [P, P])
        v0_bias = sb("v0_bias", [P, 2, C])
        work = sb("work", [P, 12, NK * D])
        raw = {n: work[:, i, :].rearrange("o (k h) -> o k h", k=NK)
               for i, n in enumerate(("q1", "k1", "v1", "o1", "q2", "k2", "v2", "o2", "q3", "k3", "v3", "o3"))}
        wT = {n: pair_of(f"wT_{n}", [P, NK, D]) for n in ("q1", "k1", "v1", "o1", "q2", "k2", "v2", "o2", "k3", "v3")}
        gamma = sb("gamma", [P, 2, NK])
        beta = sb("beta", [P, 2, NK])
        gates = sb("gates", [P, 3])
        tgates = sb("tgates", [P, 2])
        mask_u8 = sb("mask_u8", [B // 2, P], U8)
        mask_f = sb("mask_f", [B // 2, P])
        mask_col = sb("mask_col", [P, B // 2])
        mask_sum = sb("mask_sum", [P, B // 2])
        mix_col = sb("mix_col", [P, B // 2])
        half_neg = sb("half_neg", [P, 2 * NP])

        x_raw = sb("x_raw", [P, NP, D])
        c_raw = sb("c_raw", [P, NP, D])
        mrow_u8 = sb("mrow_u8", [P, NP, P], U8)
        drop_row = sb("drop_row", [P, NP, P])
        stats = sb("stats", [P, 2 * NP, 6])
        mean_var = sb("mean_var", [P, 2 * NP, 2])
        var_eps = sb("var_eps", [P, 2 * NP])
        rstd = sb("rstd", [P, 2 * NP])
        x_norm = sb("x_norm", [P, NP, D])
        c_norm = sb("c_norm", [P, NP, D])
        mask_g = sb("mask_g", [P, NP])
        mix_g = sb("mix_g", [P, NP])
        mix_tmp = drop_row
        mix = sb("mix", [P, NP, P])
        xT = sb("xT", [P, NK, TOK])
        c_tmp = sb("c_tmp", [P, NK, TOK])
        cT = pair_of("cT", [P, NK, TOK])
        aT = [pair_of(f"a{l}T", [P, NK, TOK]) for l in (1, 2)]
        mn = sb("mn", [P, NP, D])
        mm = sb("mm", [P, NP, D])
        v0 = sb("v0", [P, GB, 2, V0W])
        state = sb("state", [P, NK, TOK])
        o_sorted = [state[:, l, :].rearrange("o (m h) -> o m h", m=NK) for l in range(2)]
        state_hl = pair_of("state", [P, NK, TOK])
        kbd = sb("kbd", [P, NK, GB, 4, C])
        v2 = [sb(f"v2_{l}", [P, NP, NJ, 2, VW]) for l in (1, 2)]
        qe = work[:, 8:12, :].rearrange("p a b -> p (a b)").rearrange("p (k b q t) -> p k b q t", k=NK, b=GB, q=2)
        a_tmp = work[:, 8:12, :].rearrange("p a b -> p (a b)").rearrange("p (l k t) -> p l k t", l=2, k=NK)
        negmax = sb("negmax", [P, 2, NJ])
        shifted = sb("shifted", [P, 2, 512])
        wo3T = shifted[:, :, 0:D]
        probs = work[:, 0:4, :]
        probsT = work[:, 4:8, :]
        recip = sb("recip", [P, 2, 8])
        x_scaled = sb("x_scaled", [P, 2, 2, C])
        attn = xT[:].rearrange("t k n -> t (k n)").rearrange("t (p h j d) -> t p h j d", p=NP, h=2, j=NJ)
        attnT = pair_of("attnT", [P, 2, TOK])
        k3T = mn[:].rearrange("p a b -> p (a b)").rearrange("p (k t) -> p k t", k=NK)
        v3 = mm
        sums3 = sb("sums3", [P, 2, 2])
        recip3 = sb("recip3", [P, 2, 2])
        probs3 = sb("probs3", [P, NP, 2, C])
        result = sb("result", [P, NP, D])

        proj = [bank("proj0"), bank("proj1")]
        scores = [bank("scores0"), bank("scores1")]
        turned = [bank("turned0"), bank("turned1")]
        weighted = [bank("weighted0"), bank("weighted1")]

        proj_full, proj_free = [sem(f"proj_full{i}") for i in range(2)], [sem(f"proj_free{i}") for i in range(2)]
        scores_full, scores_free = [sem(f"scores_full{i}") for i in range(2)], [sem(f"scores_free{i}") for i in range(2)]
        turned_full, turned_free = [sem(f"turned_full{i}") for i in range(2)], [sem(f"turned_free{i}") for i in range(2)]
        weighted_full, weighted_free = [sem(f"weighted_full{i}") for i in range(2)], [sem(f"weighted_free{i}") for i in range(2)]
        w0_loaded, w3_loaded, w1_loaded, w2_loaded = sem("w0_loaded"), sem("w3_loaded"), sem("w1_loaded"), sem("w2_loaded")
        const_loaded, mask_loaded, scales_loaded = sem("const_loaded"), sem("mask_loaded"), sem("scales_loaded")
        group_loaded = sem("group_loaded")
        cleared, w0_cleared = sem("cleared"), sem("w0_cleared")
        mask_ready, mix_col_ready, mask_sum_ready = sem("mask_ready"), sem("mix_col_ready"), sem("mask_sum_ready")
        tanh_ready, bl_ready = sem("tanh_ready"), sem("bl_ready")
        pool_held, sp_held = sem("pool_held"), sem("sp_held")
        w_hi, o_sorted_ready = sem("w_hi"), sem("o_sorted_ready")
        stats_ready, mv_ready = sem("stats_ready"), sem("mv_ready")
        ve_ready, rstd_ready, normed = sem("ve_ready"), sem("rstd_ready"), sem("normed")
        drop_ready, mask_g_ready, mix_tmp_ready, mix_ready = sem("drop_ready"), sem("mask_g_ready"), sem("mix_tmp_ready"), sem("mix_ready")
        copied, front_hi, front_split = sem("copied"), sem("front_hi"), sem("front_split")
        rowmax, exps, recip_ready, state_sum, state_hi, state_split = sem("rowmax"), sem("exps"), sem("recip_ready"), sem("state_sum"), sem("state_hi"), sem("state_split")
        attn_hi, sums_ready, probs3_ready, stored = sem("attn_hi"), sem("sums_ready"), sem("probs3_ready"), sem("stored")
        result_free = sem("result_free")

        x_g = x.rearrange("(g p h) c d -> g (h c) p d", p=NP, h=2)
        c_g = ctx_in.rearrange("(g p h) c d -> g (h c) p d", p=NP, h=2)
        y_g = out.rearrange("(g q p h) c d -> g q (h c) p d", q=2, p=2, h=2)
        m_g = mask.rearrange("(g k) s -> g (k s)", k=GB)

        blk = stack.enter_context(nc.Block())

        def w_in(m):
            return m.rearrange("(k p) h -> p k h", p=P)

        @blk.sync
        def _(sp):
            def hold(signal, n):
                sp.wait_ge(signal, n)
                sp.sem_inc(sp_held, 1)

            def load_group(g):
                sp.dma_start(x_raw[:], x_g[g]).then_inc(group_loaded, 16)
                sp.dma_start(c_raw[:], c_g[g]).then_inc(group_loaded, 16)
                sp.dma_start(mrow_u8[:].rearrange("r p k -> r (p k)"),
                             m_g[g].unsqueeze(0).broadcast_to([P, TOK])).then_inc(group_loaded, 16)

            def iteration(g, last):
                if not last:
                    for i in range(2):
                        hold(proj_full[i], g * (p_n // 2) + P_BASE)
                    hold(normed, g + 1)
                    hold(drop_ready, g + 1)
                    load_group(g + 1)
                for q in range(2):
                    i, n = p_count(g, ("P", "PV", q), last)
                    hold(proj_free[i], n)
                    sp.dma_start(y_g[g, q], result[:, 2 * q:2 * q + 2, :]).then_inc(stored, 16)
                sp.wait_ge(stored, 32 * g + 32)
                sp.sem_inc(result_free, 1)

            sp.dma_start(ident[:], cst_ident).then_inc(const_loaded, 16)
            sp.dma_start(block[:], cst_block).then_inc(const_loaded, 16)
            sp.dma_start(parity[:], cst_parity).then_inc(const_loaded, 16)
            sp.dma_start(mask_u8[:], mask.rearrange("(p h) s -> p (h s)", h=2)).then_inc(mask_loaded, 16)
            sp.wait_ge(w0_cleared, 1)
            for i, n in enumerate(("Wn", "Wm", "Wo", "Wl")):
                for h in range(2):
                    sp.dma_start(w0_bd[C * h:C * h + C, i, C * h:C * h + C], w[f"L0_xattn_{n}"]).then_inc(w0_loaded, 16)
            for i, n in enumerate(("bn", "bm", "bl")):
                for h in range(2):
                    sp.dma_start(w0_cols[C * h:C * h + C, i:i + 1], w[f"L0_xattn_{n}"].unsqueeze(1)).then_inc(w0_loaded, 16)
            for h in range(2):
                sp.dma_start(bo_row[:, h, :], w["L0_xattn_bo"].unsqueeze(0).broadcast_to([P, C])).then_inc(w0_loaded, 16)
            sp.sem_inc(result_free, 1)
            load_group(0)
            with sp.Fori(0, NG - 1) as g:
                iteration(g, False)
            iteration(NG - 1, True)

        @blk.tensor
        def _(pe):
            def split_product(o, lhs, rhs, first, last):
                (lh, ll), (rh, rl) = lhs, rhs
                pe.matmul(o, lh, rh, start=first, stop=False)
                pe.matmul(o, lh, rl, start=False, stop=False)
                return pe.matmul(o, ll, rh, start=False, stop=last)

            def cut(hl, *index):
                return hl[0][index], hl[1][index]

            ALL = slice(None)

            def features_by_tokens(o, wname, m, operand):
                for k in range(NK):
                    mm_ = split_product(o, cut(wT[wname], ALL, k, slice(P * m, P * m + P)), cut(operand, ALL, k, ALL),
                                        k == 0, k == NK - 1)
                return mm_

            def tokens_by_features(o, operand, wname, p):
                for k in range(NK):
                    mm_ = split_product(o, cut(operand, ALL, k, slice(P * p, P * p + P)), cut(wT[wname], ALL, k, ALL),
                                        k == 0, k == NK - 1)
                return mm_

            def wait_copied(g, last, steps, filling=None):
                base = 0 if g is None else g * (p_n // 2)
                need = {}
                for step in steps:
                    bk, n = p_count(None if g is None else 0, step, last)
                    need[bk] = max(need.get(bk, 0), n)
                if filling:
                    bk, n = p_count(None if g is None else 0, filling, last)
                    need[bk] = max(need.get(bk, 0), n - 1)
                for bk, n in need.items():
                    if n:
                        pe.wait_ge(proj_free[bk], base + n)

            def proj_step(g, step, last):
                _, name, i = step
                bk, n = p_count(g, step, last)
                o = proj[bk]
                wait_copied(g, last, [("P", "AT" + name[1], h) for h in range(2)] if name in ("O1", "O2") and i == 0 else [],
                            filling=step)
                if name == "xT":
                    if i == 0 and g is None:
                        pe.wait_ge(group_loaded, 48)
                    elif i == 0:
                        pe.wait_ge(group_loaded, g * 48 + 96)
                    for p in range(NP):
                        mm_ = pe.transpose(o[:, P * p:P * p + P], x_raw[:, p, P * i:P * i + P], ident[:])
                elif name == "cT":
                    for p in range(NP):
                        mm_ = pe.transpose(o[:, P * p:P * p + P], c_raw[:, p, P * i:P * i + P], ident[:])
                elif name == "aT":
                    if i == 0:
                        pe.wait_ge(normed, 1 if g is None else g + 2)
                        pe.wait_ge(mix_ready, 1 if g is None else g + 2)
                    for p in range(NP):
                        mm_ = pe.matmul(o[:, P * p:P * p + P], c_norm[:, p, P * i:P * i + P], mix[:, p, :],
                                        start=True, stop=True)
                elif name in ("Mn", "Mm"):
                    src, wi = (x_norm, 0) if name == "Mn" else (c_norm, 1)
                    for q in range(2):
                        mm_ = pe.matmul(o[:, D * q:D * q + D], w0T[:, wi, :], src[:, 2 * i + q, :], start=True, stop=True)
                elif name == "V0":
                    for q in range(2):
                        for s in range(2):
                            mm_ = pe.matmul(o[:, (2 * q + s) * P:(2 * q + s + 1) * P], c_raw[:, 2 * i + q, P * s:P * s + P],
                                            wv0[:], start=True, stop=True)
                elif name in ("K1", "K2", "K3"):
                    l = int(name[1])
                    if i == 0:
                        pe.wait_ge(front_split, 6 * g + 6)
                    mm_ = features_by_tokens(o[:], f"k{l}", i, aT[l - 1] if l < 3 else cT)
                elif name in ("V1", "V2", "V3"):
                    l = int(name[1])
                    for q in range(2):
                        mm_ = tokens_by_features(o[:, D * q:D * q + D], aT[l - 1] if l < 3 else cT, f"v{l}", 2 * i + q)
                elif name in ("Q1", "Q2"):
                    l = int(name[1])
                    if i == 0:
                        pe.wait_ge(state_split, 4 * g + 2 * l)
                    mm_ = features_by_tokens(o[:], f"q{l}", i, state_hl)
                elif name in ("AT1", "AT2"):
                    for q in range(2):
                        p = 2 * i + q
                        for c in range(2):
                            ba, _, na = ring_count(g, a_at[("A", int(name[2]), p)] + c, a_n)
                            pe.wait_ge(weighted_free[ba], na)
                        for h in range(2):
                            mm_ = pe.transpose(o[:, (2 * q + h) * P:(2 * q + h + 1) * P],
                                               attn[:, p, h].rearrange("t j d -> t (j d)"), ident[:])
                elif name in ("O1", "O2"):
                    mm_ = features_by_tokens(o[:], f"o{name[1]}", i, attnT)
                elif name == "XN":
                    for q in range(2):
                        p = 2 * i + q
                        for k in range(NK):
                            mm_ = pe.transpose(o[:, D * q + P * k:D * q + P * k + P], state[:, k, P * p:P * p + P], ident[:])
                elif name == "PV":
                    bt, _, nt = ring_count(g, t_at[("T", 3, i)], t_n)
                    pe.wait_ge(turned_free[bt], nt)
                    for q in range(2):
                        p = 2 * i + q
                        mm_ = pe.matmul(o[:, D * q:D * q + D], probsT[:, i, P * q:P * q + P], v3[:, p, :], start=True, stop=True)
                mm_.then_inc(proj_full[bk], 1)

            def weight_step(step):
                name = step[1]
                bk, n = p_count(None, step, False)
                o = proj[bk]
                wait_copied(None, False, {"W0": [("P", "W0T", 0)], "VW3": [("P", "Wo3T", 0)]}.get(name, []), filling=step)
                if name == "W0T":
                    pe.wait_ge(const_loaded, 48)
                    pe.wait_ge(w0_loaded, 16 * 16)
                    pe.wait_ge(mask_ready, 1)
                    for i in range(3):
                        pe.transpose(o[:, P * i:P * i + P], w0_bd[:, i, :], ident[:])
                    mm_ = pe.transpose(o[:, 3 * P:3 * P + B // 2], mask_f[:], ident[0:B // 2, 0:B // 2])
                elif name == "W0":
                    pe.wait_ge(bl_ready, 1)
                    pe.matmul(o[:, 0:P], bl_wide[:], w0T[:, 2, :], start=True, stop=True)
                    mm_ = pe.matmul(o[:, P:2 * P], w0_bd[:, 3, :], w0T[:, 2, :], start=True, stop=True)
                elif name == "MS":
                    mm_ = pe.matmul(o[:, 0:B // 2], block[:], mask_col[:], start=True, stop=True)
                elif name == "Wo3T":
                    pe.wait_ge(w3_loaded, 64)
                    for k in range(NK):
                        for m in range(NK):
                            mm_ = pe.transpose(o[:, D * k + P * m:D * k + P * m + P], raw["o3"][:, m, P * k:P * k + P], ident[:])
                elif name == "M3":
                    for k in range(NK):
                        for m in range(NK):
                            mm_ = pe.matmul(o[:, D * k:D * k + D], raw["k3"][:, m, P * k:P * k + P], raw["q3"][:, m, :],
                                            start=m == 0, stop=m == NK - 1)
                elif name == "VW3":
                    for k in range(NK):
                        for m in range(NK):
                            mm_ = pe.matmul(o[:, D * k:D * k + D], raw["v3"][:, m, P * k:P * k + P], wo3T[:, m, :],
                                            start=m == 0, stop=m == NK - 1)
                else:
                    which, l = name[1], name[2]
                    if which == "q":
                        pe.wait_ge(w1_loaded if l == "1" else w2_loaded, 64)
                    src = raw[which + l] if which != "o" else o_sorted[int(l) - 1]
                    if which == "o":
                        pe.wait_ge(o_sorted_ready, int(l))
                    for k in range(NK):
                        for m in range(NK):
                            mm_ = pe.transpose(o[:, D * k + P * m:D * k + P * m + P], src[:, m, P * k:P * k + P], ident[:])
                mm_.then_inc(proj_full[bk], 1)

            def scores_step(g, step, last):
                _, l, i = step
                bk, n, _ = ring_count(g, s_at[step], s_n)
                o = scores[bk]
                pe.wait_ge(scores_free[bk], n)
                if l == 0:
                    if i == 0:
                        for r in range(2):
                            pe.wait_ge(proj_free[r], g * (p_n // 2) + (P_BASE - 1))
                    h = C * (i % 2)
                    for u in range(2):
                        mm_ = pe.matmul(o[:, D * u:D * u + D], mn[h:h + C, i // 2, P * u:P * u + P], mm[h:h + C, i // 2, :],
                                        start=True, stop=True)
                elif l < 3:
                    if i == 0:
                        wait_copied(g, last, [("P", f"{n}{l}", c) for n in "QK" for c in range(2)])
                    for c in range(NK):
                        mm_ = pe.matmul(o[:, D * c:D * c + D], qe[:, c, i].rearrange("p q t -> p (q t)"),
                                        kbd[:, c, i].rearrange("p r s -> p (r s)"), start=True, stop=True)
                else:
                    if i == 0:
                        wait_copied(g, last, [("P", n, c) for n in ("O2", "K3") for c in range(2)])
                    for q in range(2):
                        p = 2 * i + q
                        for k in range(NK):
                            mm_ = pe.matmul(o[:, P * q:P * q + P], state[:, k, P * p:P * p + P], k3T[:, k, P * p:P * p + P],
                                            start=k == 0, stop=k == NK - 1)
                mm_.then_inc(scores_full[bk], 1)

            def turn_step(g, step):
                _, l, i = step
                for c in range(2 if l in (1, 2) else 1):
                    bk, n, _ = ring_count(g, t_at[step] + c, t_n)
                    o = turned[bk]
                    pe.wait_ge(turned_free[bk], n)
                    if l == 0:
                        ba, _, na = ring_count(g, s_at[("S", 0, i)], s_n)
                        pe.wait_ge(scores_free[ba], na)
                        for s in range(2):
                            for u in range(2):
                                mm_ = pe.transpose(o[:, D * s + P * u:D * s + P * u + P],
                                                   probs[:, i % 4, D * u + P * s:D * u + P * s + P], ident[:])
                    elif l < 3:
                        if c == 0:
                            pe.wait_ge(exps, 18 * g + (8 * (l - 1) + 2 * i + 2))
                        e = probs[:, 2 * (i % 2):2 * (i % 2) + 2, :].rearrange("t a (j k) -> t (a j) k", k=P)
                        for j in range(4):
                            mm_ = pe.transpose(o[:, P * j:P * j + P], e[:, 4 * c + j, :], ident[:])
                    else:
                        pe.wait_ge(probs3_ready, 2 * g + (i + 1))
                        for q in range(2):
                            mm_ = pe.transpose(o[:, P * q:P * q + P], probs3[:, 2 * i + q].rearrange("t b s -> t (b s)"), ident[:])
                    mm_.then_inc(turned_full[bk], 1)

            def weighted_step(g, step, last):
                _, l, i = step
                for c in range(2 if l in (1, 2) else 1):
                    n0 = a_at[step] + c
                    bk, n, _ = ring_count(g, n0, a_n)
                    o = weighted[bk]
                    if l or i % 2 == 0:
                        pe.wait_ge(weighted_free[bk], n)
                    bt, _, nt = ring_count(g, t_at[("T", l, i)] + c, t_n)
                    pe.wait_ge(turned_free[bt], nt)
                    if l == 0:
                        if i == 0:
                            for r in range(2):
                                pe.wait_ge(proj_free[r], g * (p_n // 2) + P_BASE)
                        for u in range(2):
                            for s in range(2):
                                mm_ = pe.matmul(o[:, (2 * (i % 2) + u) * V0W:(2 * (i % 2) + u + 1) * V0W],
                                                probsT[:, i % 4, D * s + P * u:D * s + P * u + P], v0[:, i, s, :],
                                                start=s == 0, stop=s == 1)
                    else:
                        if i == 0 and c == 0:
                            wait_copied(g, last, [("P", f"V{l}", h) for h in range(2)])
                        e = probsT[:, 2 * (i % 2) + c, :].rearrange("k (j t) -> k j t", t=P)
                        for j in range(4):
                            mm_ = pe.matmul(o[:, 2 * VW * j:2 * VW * (j + 1)], e[:, j, :],
                                            v2[l - 1][:, i, 4 * c + j].rearrange("k b v -> k (b v)"), start=True, stop=True)
                    if l or i % 2:
                        mm_.then_inc(weighted_full[bk], 1)

            def iteration(g, last):
                for step in (LAST_ORDER if last else ORDER):
                    if step[0] == "P":
                        proj_step(g, step, last)
                    elif step[0] == "S":
                        scores_step(g, step, last)
                    elif step[0] == "T":
                        turn_step(g, step)
                    elif step[0] == "A":
                        weighted_step(g, step, last)

            for free in scores_free + turned_free + weighted_free:
                pe.sem_inc(free, 1)
            pe.wait_ge(cleared, 1)
            for step in WEIGHT_STEPS:
                weight_step(step)
            for step in front_order():
                proj_step(None, step, False)
            with pe.Fori(0, NG - 1) as g:
                iteration(g, False)
            iteration(NG - 1, True)

        @blk.scalar
        def _(act):
            def full(g, step, last):
                bk, n = p_count(g, step, last)
                act.wait_ge(proj_full[bk], n)
                return proj[bk], proj_free[bk]

            def proj_step(g, step, last):
                _, name, i = step
                if name == "xT":
                    o, free = full(g, step, last)
                    act.activation(xT[:, i, :], o[:], ACT.Copy).then_inc(free, 1)
                elif name == "cT":
                    o, free = full(g, step, last)
                    act.activation(c_tmp[:, i, :], o[:], ACT.Copy).then_inc(free, 1)
                elif name == "aT":
                    o, free = full(g, step, last)
                    act.activation(a_tmp[:, 0, i, :], o[:], ACT.Identity, scale=gamma[:, 0, i:i + 1],
                                   bias=beta[:, 0, i:i + 1]).then_inc(copied, 1)
                    act.activation(a_tmp[:, 1, i, :], o[:], ACT.Identity, scale=gamma[:, 1, i:i + 1],
                                   bias=beta[:, 1, i:i + 1]).then_inc(free, 1)
                elif name in ("Mn", "Mm"):
                    o, free = full(g, step, last)
                    dst, col = (mn, 0) if name == "Mn" else (mm, 1)
                    act.activation(dst[:, 2 * i:2 * i + 2, :], o[:].rearrange("c (q t) -> c q t", q=2), ACT.Identity,
                                   bias=w0_cols[:, col:col + 1]).then_inc(free, 1)
                elif name in ("K1", "K2") and i == 0:
                    o, free = full(g, step, last)
                    for r in range(4):
                        ins = act.activation(kbd[32 * r:32 * r + 32, i, :, r, :],
                                             o[32 * r:32 * r + 32, :].rearrange("p (b s) -> p b s", b=GB), ACT.Copy)
                    ins.then_inc(free, 1)
                elif name == "K3":
                    o, free = full(g, step, last)
                    act.activation(k3T[:, i, :], o[:], ACT.Copy).then_inc(free, 1)
                elif name == "V3":
                    o, free = full(g, step, last)
                    act.activation(v3[:, 2 * i:2 * i + 2, :], o[:].rearrange("s (q h) -> s q h", q=2), ACT.Copy).then_inc(free, 1)
                elif name in ("Q1", "Q2"):
                    o, free = full(g, step, last)
                    for q in range(2):
                        ins = act.activation(qe[:, i, :, q, :], o[:].rearrange("p (b t) -> p b t", b=GB), ACT.Identity,
                                             scale=parity[:, q:q + 1])
                    ins.then_inc(free, 1)
                elif name in ("AT1", "AT2"):
                    o, _ = full(g, step, last)
                    act.activation(attnT[0][:, :, TOK // 2 * i:TOK // 2 * (i + 1)].rearrange("f q (b t) -> f q b t", t=C),
                                   o[:].rearrange("f (b q t) -> f q b t", q=2, t=C), ACT.Copy).then_inc(attn_hi, 1)
                elif name == "XN":
                    o, free = full(g, step, last)
                    if i == 0:
                        act.wait_ge(result_free, g + 1)
                    act.activation(result[:, 2 * i:2 * i + 2, :], o[:].rearrange("s (q h) -> s q h", q=2), ACT.Copy).then_inc(free, 1)

            def exp_step(g, step):
                _, l, i = step
                bk, _, n = ring_count(g, s_at[("S", l, i)], s_n)
                if l == 0:
                    act.wait_ge(rowmax, 26 * g + (i + 1))
                    for u in range(2):
                        ins = act.activation(probs[:, i % 4, D * u:D * u + D], scores[bk][:, D * u:D * u + D], ACT.Exp,
                                             bias=negmax[:, i % 2, u:u + 1])
                    ins.then_inc(scores_free[bk], 1)
                elif l < 3:
                    act.wait_ge(scores_free[bk], n)
                    e = probs[:, 2 * (i // 2 % 2):2 * (i // 2 % 2) + 2, :].rearrange("t a (j h s) -> t (a j) h s", h=2, s=C)
                    act.activation(e[:, :, i % 2, :], shifted[:, i % 2, :].rearrange("t (j s) -> t j s", s=C),
                                   ACT.Exp).then_inc(exps, 1)
                else:
                    act.wait_ge(scores_free[bk], n)
                    act.activation(probs[:, i, 0:P], shifted[:, i, 0:P], ACT.Exp).then_inc(exps, 1)

            def turn_step(g, step):
                _, l, i = step
                for c in range(2 if l in (1, 2) else 1):
                    bk, n, _ = ring_count(g, t_at[step] + c, t_n)
                    act.wait_ge(turned_full[bk], n)
                    slot = i % 4 if l == 0 else 2 * (i % 2) + c if l < 3 else i
                    width = 512 if l < 3 else D
                    act.activation(probsT[:, slot, 0:width], turned[bk][:, 0:width], ACT.Copy).then_inc(turned_free[bk], 1)

            def weight_step(step):
                name = step[1]
                if name in ("W0T", "W0", "MS"):
                    return
                o, free = full(None, step, False)
                v = o[:].rearrange("h (k m) -> h k m", k=NK)
                if name == "Wo3T":
                    act.wait_ge(const_loaded, 48)
                    act.activation(wo3T, v, ACT.Identity, scale=gates[:, 2:3]).then_inc(free, 1)
                elif name == "M3":
                    act.activation(wT["k3"][0][:], v, ACT.Copy, scale=D ** -0.5).then_inc(w_hi, 1)
                elif name == "VW3":
                    act.activation(wT["v3"][0][:], v, ACT.Copy).then_inc(w_hi, 1)
                else:
                    which, l = name[1], int(name[2])
                    if which == "o":
                        act.activation(wT[which + name[2]][0][:], v, ACT.Identity, scale=tgates[:, l - 1:l]).then_inc(w_hi, 1)
                    else:
                        act.activation(wT[which + name[2]][0][:], v, ACT.Copy).then_inc(w_hi, 1)

            def iteration(g, last):
                for step in (LAST_ORDER if last else ORDER):
                    if step[0] == "P":
                        proj_step(g, step, last)
                    elif step[0] == "X":
                        exp_step(g, step)
                    elif step[0] == "T":
                        turn_step(g, step)

            for l in (1, 2):
                for n in "qkvo":
                    act.dma_start(raw[n + str(l)][:], w_in(w[f"L{l}_xattn_W{n}"])).then_inc((w1_loaded, w2_loaded)[l - 1], 16)
            act.wait_ge(scales_loaded, 11 * 16)
            act.activation(tgates[:], gates[:, 0:2], ACT.Tanh).then_inc(tanh_ready, 1)
            act.wait_ge(tanh_ready, 1)
            for step in WEIGHT_STEPS:
                weight_step(step)
            for step in front_order():
                proj_step(None, step, False)
            with act.Fori(0, NG - 1) as g:
                iteration(g, False)
            iteration(NG - 1, True)

        @blk.vector
        def _(dve):
            def full(g, step, last):
                bk, n = p_count(g, step, last)
                dve.wait_ge(proj_full[bk], n)
                return proj[bk], proj_free[bk], n

            def proj_step(g, step, last):
                _, name, i = step
                if name == "V0":
                    o, free, _ = full(g, step, last)
                    for q in range(2):
                        b = 4 * i + 2 * q
                        ins = dve.tensor_tensor(v0[:, b:b + 2, :, 0:C].rearrange("k b s c -> k s b c"),
                                                o[:, D * q:D * q + D].rearrange("k (s b c) -> k s b c", s=2, b=2),
                                                v0_bias[:].unsqueeze(1).broadcast_to([P, 2, 2, C]), ALU.add)
                    ins.then_inc(free, 1)
                elif name in ("K1", "K2") and i == 1:
                    o, free, _ = full(g, step, last)
                    for r in range(4):
                        ins = dve.tensor_copy(kbd[32 * r:32 * r + 32, i, :, r, :],
                                              o[32 * r:32 * r + 32, :].rearrange("p (b s) -> p b s", b=GB))
                    ins.then_inc(free, 1)
                elif name in ("V1", "V2"):
                    o, free, _ = full(g, step, last)
                    dst = v2[int(name[1]) - 1]
                    for h in range(2):
                        rows = slice(C * h, C * h + C)
                        m = mask_g[rows, 2 * i:2 * i + 2]
                        dve.tensor_copy(dst[rows, 2 * i:2 * i + 2, :, h, VW - 1], m.unsqueeze(2).broadcast_to([C, 2, NJ]))
                        ins = dve.tensor_tensor(dst[rows, 2 * i:2 * i + 2, :, h, 0:VW - 1],
                                                o[rows, :].rearrange("k (q j v) -> k q j v", q=2, j=NJ),
                                                m.unsqueeze(2).unsqueeze(3).broadcast_to([C, 2, NJ, VW - 1]), ALU.mult)
                    ins.then_inc(free, 1)
                elif name in ("AT1", "AT2"):
                    o, free, _ = full(g, step, last)
                    dve.wait_ge(attn_hi, 4 * g + (2 * int(name[2]) - 1 + i))
                    cols = slice(TOK // 2 * i, TOK // 2 * (i + 1))
                    dve.tensor_tensor(attnT[1][:, :, cols].rearrange("f q (b t) -> f q b t", t=C),
                                      o[:].rearrange("f (b q t) -> f q b t", q=2, t=C),
                                      attnT[0][:, :, cols].bitcast(F32).rearrange("f q (b t) -> f q b t", t=C),
                                      ALU.subtract).then_inc(free, 1)
                elif name in ("O1", "O2"):
                    o, free, n = full(g, step, last)
                    dve.tensor_tensor(state[:, i, :], o[:], state[:, i, :], ALU.add).then_inc(free, 1)
                    if name == "O1":
                        dve.wait_ge(free, n)
                        dve.tensor_copy(state_hl[0][:, i, :], state[:, i, :]).then_inc(state_hi, 1)
                        dve.wait_ge(state_hi, 4 * g + (3 + i))
                        dve.tensor_tensor(state_hl[1][:, i, :], state[:, i, :], state_hl[0][:, i, :].bitcast(F32),
                                          ALU.subtract).then_inc(state_split, 1)
                elif name == "PV":
                    o, free, _ = full(g, step, last)
                    bx, nx = p_count(g, ("P", "XN", i), last)
                    dve.wait_ge(proj_free[bx], nx)
                    r = result[:, 2 * i:2 * i + 2, :]
                    dve.tensor_tensor(r, o[:].rearrange("s (q h) -> s q h", q=2), r, ALU.add).then_inc(free, 1)

            def scores_step(g, step):
                _, l, i = step
                bk, n, _ = ring_count(g, s_at[step], s_n)
                s = scores[bk]
                dve.wait_ge(scores_full[bk], n)
                if l == 0:
                    if i >= 2:
                        bx, _, nx = ring_count(g, s_at[("S", 0, i - 2)], s_n)
                        dve.wait_ge(scores_free[bx], nx)
                    dve.tensor_reduce(negmax[:, i % 2, 0:2], s[:].rearrange("t (u k) -> t u k", u=2), AX_X, ALU.max,
                                      negate=True).then_inc(rowmax, 1)
                elif l < 3:
                    sv = s[:].rearrange("t (j k) -> t j k", k=C)
                    dve.tensor_reduce(negmax[:, i % 2, :], sv, AX_X, ALU.max, negate=True).then_inc(rowmax, 1)
                    if i >= 2:
                        dve.wait_ge(exps, 18 * g + (8 * (l - 1) + i - 1))
                    dve.wait_ge(rowmax, 26 * g + (8 * l + i + 1))
                    dve.tensor_tensor(shifted[:, i % 2, :].rearrange("t (j k) -> t j k", k=C), sv,
                                      negmax[:, i % 2, :].unsqueeze(2).broadcast_to([P, NJ, C]),
                                      ALU.add).then_inc(scores_free[bk], 1)
                else:
                    sv = s[:, 0:2 * P].rearrange("t (q h k) -> t q h k", q=2, h=2)
                    for h in range(2):
                        rows = slice(C * h, C * h + C)
                        ins = dve.tensor_reduce(negmax[rows, i, 0:2], sv[rows, :, h, :], AX_X, ALU.max, negate=True)
                    ins.then_inc(rowmax, 1)
                    dve.wait_ge(rowmax, 26 * g + (25 + i))
                    for h in range(2):
                        rows = slice(C * h, C * h + C)
                        ins = dve.tensor_tensor(shifted[rows, i, 0:P].rearrange("t (q k) -> t q k", q=2), sv[rows, :, h, :],
                                                negmax[rows, i, 0:2].unsqueeze(2).broadcast_to([C, 2, C]), ALU.add)
                    ins.then_inc(scores_free[bk], 1)

            def normalise3(g, i):
                e = probs[:, i, 0:P].rearrange("t (q k) -> t q k", q=2)
                dve.wait_ge(exps, 18 * g + (17 + i))
                dve.reduce_sum(sums3[:, i, :], e, AX_X).then_inc(sums_ready, 1)
                dve.wait_ge(sums_ready, 2 * g + (i + 1))
                dve.reciprocal(recip3[:, i, :], sums3[:, i, :]).then_inc(recip_ready, 1)
                dve.wait_ge(recip_ready, 22 * g + (21 + i))
                for h in range(2):
                    rows = slice(C * h, C * h + C)
                    ins = dve.tensor_tensor(probs3[rows, 2 * i:2 * i + 2, h, :], e[rows],
                                            recip3[rows, i, :].unsqueeze(2).broadcast_to([C, 2, C]), ALU.mult)
                ins.then_inc(probs3_ready, 1)

            def weighted_step(g, step):
                _, l, i = step
                if l == 0:
                    if i % 2 == 0:
                        return
                    n0 = a_at[step]
                    bk, n, released = ring_count(g, n0, a_n)
                    p = i // 2
                    dve.wait_ge(weighted_full[bk], n)
                    sums = weighted[bk][:, 0:4 * V0W].rearrange("t (h u v) -> t h u v", h=2, u=2)
                    rz = recip[:, bk, 0:4].rearrange("t (h u) -> t h u", h=2)
                    dve.reciprocal(rz, sums[:, :, :, C]).then_inc(recip_ready, 1)
                    dve.wait_ge(recip_ready, 22 * g + (p + 1))
                    dve.tensor_tensor(x_scaled[:], sums[:, :, :, 0:C], rz.unsqueeze(3).broadcast_to([P, 2, 2, C]),
                                      ALU.mult).then_inc(weighted_free[bk], 1)
                    dve.wait_ge(weighted_free[bk], released)
                    toks = slice(P * p, P * p + P)
                    dve.tensor_tensor(state[:, :, toks].rearrange("f u (h c) -> f h u c", h=2), x_scaled[:],
                                      xT[:, :, toks].rearrange("f u (h c) -> f h u c", h=2), ALU.add).then_inc(state_sum, 1)
                    if p % 2:
                        half = slice(TOK // 2 * (p // 2), TOK // 2 * (p // 2 + 1))
                        dve.wait_ge(state_sum, 4 * g + (p + 1))
                        dve.tensor_copy(state_hl[0][:, :, half], state[:, :, half]).then_inc(state_hi, 1)
                        dve.wait_ge(state_hi, 4 * g + (p // 2 + 1))
                        dve.tensor_tensor(state_hl[1][:, :, half], state[:, :, half], state_hl[0][:, :, half].bitcast(F32),
                                          ALU.subtract).then_inc(state_split, 1)
                    return
                for c in range(2):
                    n0 = a_at[step] + c
                    bk, n, _ = ring_count(g, n0, a_n)
                    dve.wait_ge(weighted_full[bk], n)
                    sums = weighted[bk][:, 0:4 * 2 * VW].rearrange("t (j h v) -> t j h v", j=4, h=2)
                    rz = recip[:, bk, :].rearrange("t (j h) -> t j h", j=4)
                    dve.reciprocal(rz, sums[:, :, :, VW - 1]).then_inc(recip_ready, 1)
                    dve.wait_ge(recip_ready, 22 * g + (4 + 8 * (l - 1) + 2 * i + c + 1))
                    for q in range(2):
                        rows = slice(C * q, C * q + C)
                        ins = dve.tensor_tensor(attn[rows, i, :, 4 * c:4 * c + 4, :].rearrange("t h j d -> t j h d"),
                                                sums[rows, :, :, HD * q:HD * q + HD],
                                                rz[rows].unsqueeze(3).broadcast_to([C, 4, 2, HD]), ALU.mult)
                    ins.then_inc(weighted_free[bk], 1)

            def stats_step(g, p):
                if p == 0:
                    dve.wait_ge(group_loaded, 48 if g is None else 48 * g + 96)
                for t, src in ((p, x_raw), (NP + p, c_raw)):
                    ins = dve.bn_stats(stats[:, t, :], src[:, p, :])
                ins.then_inc(stats_ready, 1)

            def mix_step(g):
                first = slice(0, NP) if g is None else bass.ds(NP * g + NP, NP)
                dve.tensor_copy(mask_g[:], mask_col[:, first]).then_inc(mask_g_ready, 1)
                dve.tensor_copy(mix_g[:], mix_col[:, first]).then_inc(mask_g_ready, 1)
                dve.wait_ge(mask_g_ready, 2 if g is None else 2 * g + 4)
                dve.wait_ge(drop_ready, 1 if g is None else g + 2)
                dve.wait_ge(stats_ready, NP if g is None else NP * g + 2 * NP)
                for p in range(NP):
                    ins = dve.scalar_tensor_tensor(out=mix_tmp[:, p, :], in0=block[:], scalar=mix_g[:, p:p + 1],
                                                   in1=drop_row[:, p, :], op0=ALU.mult, op1=ALU.mult)
                ins.then_inc(mix_tmp_ready, 1)
                for t in range(2 * NP):
                    ins = dve.bn_aggr(mean_var[:, t, :], stats[:, t, :])
                ins.then_inc(mv_ready, 1)
                dve.wait_ge(mix_tmp_ready, 1 if g is None else g + 2)
                for p in range(NP):
                    ins = dve.scalar_tensor_tensor(out=mix[:, p, :], in0=ident[:], scalar=mask_g[:, p:p + 1],
                                                   in1=mix_tmp[:, p, :], op0=ALU.mult, op1=ALU.add)
                ins.then_inc(mix_ready, 1)

            def weight_step(step):
                name = step[1]
                if name == "Wo3T":
                    return
                o, free, n = full(None, step, False)
                if name == "W0T":
                    dve.tensor_copy(mask_col[:], o[:, 3 * P:3 * P + B // 2])
                    dve.tensor_copy(w0T[:], o[:, 0:3 * P].rearrange("a (i b) -> a i b", i=3)).then_inc(free, 1)
                elif name == "W0":
                    dve.tensor_tensor(v0_bias[:], o[:, 0:P].rearrange("k (h c) -> k h c", h=2), bo_row[:], ALU.add)
                    dve.tensor_copy(wv0[:], o[:, P:2 * P]).then_inc(free, 1)
                elif name == "MS":
                    dve.tensor_scalar(mask_sum[:], o[:, 0:B // 2], 0.5, None, ALU.max).then_inc(free, 1)
                    dve.wait_ge(free, n)
                    dve.reciprocal(mix_col[:], mask_sum[:]).then_inc(mask_sum_ready, 1)
                    dve.wait_ge(mask_sum_ready, 1)
                    dve.tensor_tensor(mix_col[:], mix_col[:], mask_col[:], ALU.mult).then_inc(mix_col_ready, 1)
                    dve.wait_ge(mix_col_ready, 1)
                else:
                    v = o[:].rearrange("h (k m) -> h k m", k=NK)
                    key = {"M3": "k3", "VW3": "v3"}.get(name, name[1:])
                    hi, lo = wT[key]
                    dve.wait_ge(w_hi, WEIGHT_STEPS.index(step) - 3)
                    scalar = D ** -0.5 if name == "M3" else tgates[:, int(name[2]) - 1:int(name[2])] if name[1] == "o" else 1.0
                    dve.scalar_tensor_tensor(out=lo[:], in0=v, scalar=scalar, in1=hi[:].bitcast(F32), op0=ALU.mult,
                                             op1=ALU.subtract).then_inc(free, 1)

            def iteration(g, last):
                for step in (LAST_ORDER if last else ORDER):
                    if step[0] == "P":
                        proj_step(g, step, last)
                    elif step[0] == "S":
                        scores_step(g, step)
                    elif step[0] == "X" and step[1] == 3:
                        normalise3(g, step[2])
                    elif step[0] == "A":
                        weighted_step(g, step)
                    elif step[0] == "ST":
                        stats_step(g, step[1])
                    elif step[0] == "MG":
                        mix_step(g)

            dve.wait_ge(mask_loaded, 16)
            dve.tensor_copy(mask_f[:], mask_u8[:]).then_inc(mask_ready, 1)
            dve.wait_ge(w0_loaded, 16 * 16)
            dve.tensor_copy(bl_wide[:], w0_cols[:, 2:3].broadcast_to([P, P])).then_inc(bl_ready, 1)
            dve.wait_ge(tanh_ready, 1)
            for step in WEIGHT_STEPS[:3]:
                weight_step(step)
            for p in range(NP):
                stats_step(None, p)
            mix_step(None)
            for l, loaded in ((1, w1_loaded), (2, w2_loaded)):
                dve.wait_ge(loaded, 64)
                for m in range(NK):
                    ins = dve.tensor_copy(o_sorted[l - 1][:, m, :].rearrange("o (q j d) -> o q j d", q=2, d=HD),
                                          raw[f"o{l}"][:, m, :].rearrange("o (j q d) -> o q j d", q=2, d=HD))
                ins.then_inc(o_sorted_ready, 1)
            for step in WEIGHT_STEPS[3:]:
                weight_step(step)
            for step in front_order():
                proj_step(None, step, False)
            with dve.Fori(0, NG - 1) as g:
                iteration(g, False)
            iteration(NG - 1, True)

        @blk.gpsimd
        def _(pool):
            def hold(signal, n):
                pool.wait_ge(signal, n)
                pool.sem_inc(pool_held, 1)

            def front(g):
                nth = 1 if g is None else g + 2
                hold(group_loaded, 48 * nth)
                if g is not None:
                    hold(mix_ready, nth - 1)
                pool.tensor_scalar(drop_row[:], mrow_u8[:], -1.0, 1.0, ALU.mult, ALU.add).then_inc(drop_ready, 1)
                hold(mv_ready, nth)
                pool.tensor_scalar(var_eps[:], mean_var[:, :, 1], EPS, None, ALU.add).then_inc(ve_ready, 1)
                pool.wait_ge(ve_ready, nth)
                pool.tensor_tensor(rstd[:], var_eps[:], half_neg[:], ALU.pow).then_inc(rstd_ready, 1)
                hold(rstd_ready, nth)
                for t in list(range(NP, 2 * NP)) + list(range(NP)):
                    src, dst = (x_raw, x_norm) if t < NP else (c_raw, c_norm)
                    ins = pool.tensor_scalar(dst[:, t % NP, :], src[:, t % NP, :], mean_var[:, t, 0:1], rstd[:, t:t + 1],
                                             ALU.subtract, ALU.mult)
                ins.then_inc(normed, 1)
                n = 0
                for name, i in (("cT", 0), ("cT", 1), ("aT", 0), ("aT", 1)):
                    bk, count = p_count(g, ("P", name, i), False)
                    hold(proj_free[bk], count)
                    for src, (hi, lo) in [(c_tmp[:, i, :], cT)] if name == "cT" else [(a_tmp[:, l, i, :], aT[l]) for l in range(2)]:
                        n += 1
                        pool.tensor_copy(hi[:, i, :], src).then_inc(front_hi, 1)
                        pool.wait_ge(front_hi, 6 * (nth - 1) + n)
                        pool.tensor_tensor(lo[:, i, :], src, hi[:, i, :].bitcast(F32), ALU.subtract).then_inc(front_split, 1)

            pool.memset(w0_bd[:], 0.0).then_inc(w0_cleared, 1)
            for n in "qkvo":
                pool.dma_start(raw[n + "3"][:], w_in(w[f"L3_xattn_w_{n}"])).then_inc(w3_loaded, 16)
            for l in (1, 2):
                for k in range(NK):
                    half = slice(P * k, P * k + P)
                    pool.dma_start(gamma[:, l - 1, k:k + 1], w[f"L{l}_xattn_ln_gamma"][half].unsqueeze(1)).then_inc(scales_loaded, 16)
                    pool.dma_start(beta[:, l - 1, k:k + 1], w[f"L{l}_xattn_ln_beta"][half].unsqueeze(1)).then_inc(scales_loaded, 16)
                pool.dma_start(gates[:, l - 1:l], w[f"L{l}_xattn_gate"].unsqueeze(0).broadcast_to([P, 1])).then_inc(scales_loaded, 16)
            pool.dma_start(gates[:, 2:3], w["L3_xattn_alpha"].unsqueeze(0).broadcast_to([P, 1])).then_inc(scales_loaded, 16)
            pool.memset(half_neg[:], -0.5)
            for t in (kbd, v2[0], v2[1], probs3):
                pool.memset(t[:], 0.0)
            pool.memset(v0[:, :, :, C], 1.0).then_inc(cleared, 1)
            pool.wait_ge(cleared, 1)
            front(None)
            with pool.Fori(0, NG - 1) as g:
                front(g)


_WEIGHTS = ['L0_xattn_Wn', 'L0_xattn_bn', 'L0_xattn_Wm', 'L0_xattn_bm', 'L0_xattn_Wl', 'L0_xattn_bl', 'L0_xattn_Wo',
            'L0_xattn_bo', 'L1_xattn_Wq', 'L1_xattn_Wk', 'L1_xattn_Wv', 'L1_xattn_Wo', 'L1_xattn_ln_gamma',
            'L1_xattn_ln_beta', 'L1_xattn_gate', 'L2_xattn_Wq', 'L2_xattn_Wk', 'L2_xattn_Wv', 'L2_xattn_Wo',
            'L2_xattn_ln_gamma', 'L2_xattn_ln_beta', 'L2_xattn_gate', 'L3_xattn_w_q', 'L3_xattn_w_k', 'L3_xattn_w_v',
            'L3_xattn_w_o', 'L3_xattn_alpha']


def kernel(**inputs):
    import numpy as _np
    import concourse.bacc as _bacc
    from concourse import mybir as _mybir
    from concourse.bass_utils import run_bass_kernel_spmd as _run

    nc = _bacc.Bacc("TRN2", target_bir_lowering=False, num_devices=1)
    arrays = {}

    def dram(name, a):
        a = _np.ascontiguousarray(a)
        arrays[f"in_{name}_dram"] = a
        return nc.dram_tensor(f"in_{name}_dram", a.shape, _mybir.dt.from_np(a.dtype), kind="ExternalInput").ap()

    x = dram("x", inputs["x"])
    ctx = dram("ctx_2048", inputs["ctx_2048"])
    mask = dram("mask", _np.asarray(inputs["mask_BxS2_bf1"]).view(_np.uint8))
    w = {n: dram(n, _np.asarray(inputs[n]).reshape(1) if _np.ndim(inputs[n]) == 0 else inputs[n]) for n in _WEIGHTS}
    rows = _np.arange(P)
    ident = dram("ident", _np.eye(P, dtype=_np.float32))
    block = dram("block", (rows[:, None] // C == rows[None, :] // C).astype(_np.float32))
    parity = dram("parity", ((rows[:, None] // HD % 2 == _np.arange(2)[None, :]) * HD ** -0.5).astype(_np.float32))
    y = nc.dram_tensor("out_0_dram", (B, C, D), F32, kind="ExternalOutput").ap()
    build(nc, x, ctx, mask, w, ident, block, parity, y)
    r = _run(nc, [arrays], core_ids=[0])
    return r.results[0]["out_0_dram"]
```

```python
from contextlib import ExitStack

import concourse.bass as bass
from concourse import mybir

F32 = mybir.dt.float32
F32R = mybir.dt.float32r
U8 = mybir.dt.uint8
ALU = mybir.AluOpType
ACT = mybir.ActivationFunctionType
AX_X = mybir.AxisListType.X

P = 128
B, C, D = 64, 64, 256
NH, HD = 16, 16
GB = 8
NG = B // GB
NP = GB // 2
TOK = GB * C
HALF = TOK // 2
NK = D // P
NJ = NH // 2
EPS = 1e-5
VW = HD * 2 + 1
V0W = C + 1


def group_order(front):
    def p(name, i):
        return [("P", name, i)]

    def at(kind, l, *i):
        return [(kind, l, n) for n in i]

    def S(l, i):
        return at("S", l, i)

    def X(l, i):
        return at("X", l, i)

    def T(l, i):
        return at("T", l, i)

    def A(l, i):
        return at("A", l, i)

    def nxt(step):
        return [step] if front else []

    f = front_order() if front else [[]] * 12
    f = [[s] if s else [] for s in f]
    o = [("SC", 0)]
    o += S(0, 0) + S(0, 1) + X(0, 0) + p("K1", 0) + T(0, 0)
    for b in range(2, GB):
        o += S(0, b) + X(0, b - 1) + A(0, b - 2) + T(0, b - 1)
        o += {3: p("K1", 1), 6: p("Q1", 0), 7: X(0, 7) + p("V1", 0)}.get(b, [])
        o += nxt(("ST", b // 2 - 1)) if b % 2 else []
    o += S(1, 0) + A(0, 6) + T(0, 7) + S(1, 1) + X(1, 0) + p("V1", 1) + A(0, 7) + nxt(("ST", 3)) + nxt(("MV", 0))
    o += S(1, 2) + X(1, 1) + p("K2", 0) + S(1, 3) + p("Q1", 1) + T(1, 0) + X(1, 2) + p("K2", 1)
    o += A(1, 0) + S(1, 4) + X(1, 3) + S(1, 5) + T(1, 1) + X(1, 4)
    o += S(1, 6) + A(1, 1) + X(1, 5) + S(1, 7) + T(1, 2) + X(1, 6) + p("V2", 0) + p("AT1", 0)
    o += A(1, 2) + X(1, 7) + p("O1", 0) + T(1, 3) + p("V2", 1) + p("Q2", 0)
    o += A(1, 3) + S(2, 0) + S(2, 1) + X(2, 0) + p("AT1", 1) + p("K3", 0)
    o += S(2, 2) + X(2, 1) + p("O1", 1) + S(2, 3) + T(2, 0) + X(2, 2) + p("K3", 1) + p("Q2", 1)
    o += A(2, 0) + S(2, 4) + X(2, 3) + S(2, 5) + T(2, 1) + X(2, 4)
    o += S(2, 6) + A(2, 1) + X(2, 5) + S(2, 7) + T(2, 2) + X(2, 6) + p("V3", 0) + p("AT2", 0)
    o += A(2, 2) + X(2, 7) + p("O2", 0) + T(2, 3) + p("V3", 1)
    o += A(2, 3) + S(3, 0) + p("AT2", 1) + f[0] + f[1] + p("O2", 1) + X(3, 0) + f[2] + f[3]
    o += S(3, 1) + T(3, 0) + p("XN", 0) + X(3, 1) + f[4] + f[5] + p("XN", 1) + T(3, 1) + p("PV", 0) + f[6] + f[7]
    return o + p("PV", 1) + f[8] + f[9] + f[10] + f[11]


def front_order():
    return [("P", n, i) for n in ("xT", "cT", "nT", "Mn", "Mm", "V0") for i in range(2)]


WEIGHT_STEPS = [("P", n, 0) for n in ("W0T", "W0", "MS", "Wo3T", "M3", "VW3")] + \
    [("P", f"{n}{l}", 0) for l in (1, 2) for n in ("Wq", "Wk", "Wv", "VB", "Wo")]


def build(nc, x, ctx_in, mask, w, cst_ident, cst_block, cst_parity, cst_own_slot, out):
    ORDER = group_order(True)
    LAST_ORDER = group_order(False)
    PROLOGUE = WEIGHT_STEPS + front_order()

    def numbered(order, kind):
        n, at = 0, {}
        for s in order:
            if kind == "A" and s[0] == "A" and s[1] == 0:
                at[s] = n
                n += s[2] % 2
            elif s[0] == kind:
                per = {"T": {1: 2, 2: 2}, "A": {1: 2, 2: 2}}.get(kind, {}).get(s[1], 1)
                at[s] = n
                n += per
        return at, n

    p_at, p_n = numbered(ORDER, "P")
    p_at_last, _ = numbered(LAST_ORDER, "P")
    p_at_pro, p_n_pro = numbered(PROLOGUE, "P")
    s_at, s_n = numbered(ORDER, "S")
    t_at, t_n = numbered(ORDER, "T")
    a_at, a_n = numbered(ORDER, "A")
    assert p_n % 2 == 0 and p_n_pro % 2 == 0 and s_n % 2 == 0 and t_n % 2 == 0 and a_n % 2 == 0
    P_BASE = p_n_pro // 2

    def p_count(g, step, last):
        if g is None:
            n = p_at_pro[step]
            return n % 2, n // 2 + 1
        n = (p_at_last if last else p_at)[step]
        return n % 2, g * (p_n // 2) + (P_BASE + n // 2 + 1)

    def ring_count(g, n, total):
        fills = g * (total // 2) + (n // 2 + 1)
        return n % 2, fills, g * (total // 2) + (n // 2 + 2)

    with ExitStack() as stack:
        def sb(name, shape, dt=F32):
            return stack.enter_context(nc.sbuf_tensor(name, shape, dt))

        def pair_of(name, shape):
            return sb(name + "_hi", shape, F32R), sb(name + "_lo", shape, F32R)

        def sem(name):
            return stack.enter_context(nc.semaphore(name))

        def bank(name):
            return stack.enter_context(nc.psum_tensor(name, [P, 512], F32))

        ident = sb("ident", [P, P])
        block = sb("block", [P, P])
        own_slot = sb("own_slot", [P, 4])
        parity = sb("parity", [P, 2])
        w0_cols = sb("w0_cols", [P, 3])
        w0T = sb("w0T", [P, 3, P])
        wv0 = sb("wv0", [P, P])
        v0_bias = sb("v0_bias", [P, 2, C])
        work = sb("work", [P, 12, NK * D])
        raw = {n: work[:, i, :].rearrange("o (k h) -> o k h", k=NK)
               for i, n in enumerate(("q1", "k1", "v1", "o1", "q2", "k2", "v2", "o2", "q3", "k3", "v3", "o3"))}
        wT = {n: pair_of(f"wT_{n}", [P, NK, D]) for n in ("q1", "k1", "v1", "o1", "q2", "k2", "v2", "o2", "k3", "v3")}
        gamma = sb("gamma", [P, 2, NK])
        k_bias = sb("k_bias", [P, 2, NK])
        v_bias = sb("v_bias", [P, 2, NK])
        o_bias = sb("o_bias", [P, 2, NK])
        gates = sb("gates", [P, 3])
        tgates = sb("tgates", [P, 2])
        mask_u8 = sb("mask_u8", [B // 2, P], U8)
        mask_f = sb("mask_f", [B // 2, P])
        mask_col = sb("mask_col", [P, B // 2])
        mask_sum = sb("mask_sum", [P, B // 2])
        mix_col = sb("mix_col", [P, B // 2])
        half_neg = sb("half_neg", [P, 2 * NP])

        x_raw = sb("x_raw", [P, NP, D])
        c_raw = sb("c_raw", [P, NP, D])
        mrow_u8 = sb("mrow_u8", [P, NP, P], U8)
        drop_row = sb("drop_row", [P, NP, P])
        stats = sb("stats", [P, 2 * NP, 6])
        mean_var = sb("mean_var", [P, 2 * NP, 2])
        var_eps = sb("var_eps", [P, 2 * NP])
        rstd = sb("rstd", [P, 2 * NP])
        x_norm = sb("x_norm", [P, NP, D])
        c_norm = sb("c_norm", [P, NP, D])
        mix = sb("mix", [P, NP, P])
        xT = sb("xT", [P, NK, TOK])
        cT = pair_of("cT", [P, NK, TOK])
        nT = pair_of("nT", [P, NK, TOK])
        mn = sb("mn", [P, NP, D])
        mm = sb("mm", [P, NP, D])
        v0 = sb("v0", [P, GB, 2, V0W])
        state = sb("state", [P, NK, TOK])
        o_sorted = [state[:, l, :].rearrange("o (m h) -> o m h", m=NK) for l in range(2)]
        state_hl = pair_of("state", [P, NK, HALF])
        kbd = [sb(f"kbd{l}", [P, NK, GB, 4, C]) for l in (1, 2)]
        k_tmp = sb("k_tmp", [P, NK, TOK])
        w0_bd = kbd[0][:, 0, 0:2].rearrange("p a b c -> p (a b c)").rearrange("p (i b) -> p i b", i=4)
        beta_row = kbd[1][:, 0, 0:2].rearrange("p a b c -> p (a b c)").rearrange("p (l h) -> p l h", l=2)
        v2 = [sb(f"v2_{l}", [P, NP, NJ, 2, VW]) for l in (1, 2)]
        qe = work[:, 8:12, :].rearrange("p a b -> p (a b)").rearrange("p (k b q t) -> p k b q t", k=NK, b=GB, q=2)
        negmax = sb("negmax", [P, 2, NJ])
        shifted = sb("shifted", [P, 2, 512])
        wo3T = shifted[:, :, 0:D]
        probs = work[:, 0:4, :]
        probsT = work[:, 4:8, :]
        recip = sb("recip", [P, 2, 8])
        x_scaled = sb("x_scaled", [P, 2, 2, C])
        attn = xT[:].rearrange("t k n -> t (k n)").rearrange("t (p h j d) -> t p h j d", p=NP, h=2, j=NJ)
        attnT = pair_of("attnT", [P, 2, HALF])
        k3T = sb("k3T", [P, NK, TOK])
        v3 = sb("v3", [P, NP, D])
        sums3 = sb("sums3", [P, 2, 2])
        recip3 = sb("recip3", [P, 2, 2])
        probs3 = sb("probs3", [P, NP, 2, C])
        result = sb("result", [P, NP, D])
        v_bias_wide = result[:, 2:4, :].rearrange("p l (m c) -> p l m c", m=NK)
        bias_product = shifted[:, :, D:2 * D]
        bl_wide, bo_row = result[:, 0, 0:P], result[:, 1, 0:P].rearrange("p (h c) -> p h c", h=2)

        proj = [bank("proj0"), bank("proj1")]
        scores = [bank("scores0"), bank("scores1")]
        turned = [bank("turned0"), bank("turned1")]
        weighted = [bank("weighted0"), bank("weighted1")]

        proj_full, proj_free = [sem(f"proj_full{i}") for i in range(2)], [sem(f"proj_free{i}") for i in range(2)]
        scores_full, scores_free = [sem(f"scores_full{i}") for i in range(2)], [sem(f"scores_free{i}") for i in range(2)]
        turned_full, turned_free = [sem(f"turned_full{i}") for i in range(2)], [sem(f"turned_free{i}") for i in range(2)]
        weighted_full, weighted_free = [sem(f"weighted_full{i}") for i in range(2)], [sem(f"weighted_free{i}") for i in range(2)]
        w0_loaded, w3_loaded, w1_loaded, w2_loaded = sem("w0_loaded"), sem("w3_loaded"), sem("w1_loaded"), sem("w2_loaded")
        const_loaded, mask_loaded, scales_loaded = sem("const_loaded"), sem("mask_loaded"), sem("scales_loaded")
        group_loaded = sem("group_loaded")
        cleared, w0_cleared = sem("cleared"), sem("w0_cleared")
        mask_ready, mix_col_ready, mask_sum_ready = sem("mask_ready"), sem("mix_col_ready"), sem("mask_sum_ready")
        tanh_ready, bl_ready = sem("tanh_ready"), sem("bl_ready")
        pool_held, sp_held, dve_held, act_held = sem("pool_held"), sem("sp_held"), sem("dve_held"), sem("act_held")
        sum_columns_ready = sem("sum_columns_ready")
        w_hi, o_sorted_ready = sem("w_hi"), sem("o_sorted_ready")
        stats_ready, mv_ready = sem("stats_ready"), sem("mv_ready")
        ve_ready, rstd_ready, normed = sem("ve_ready"), sem("rstd_ready"), sem("normed")
        mix_step, mix_ready = sem("mix_step"), sem("mix_ready")
        ctx_hi, k_spread = sem("ctx_hi"), sem("k_spread")
        bias_step, o_bias_ready = sem("bias_step"), sem("o_bias_ready")
        rowmax, exps, recip_ready, state_sum, state_hi, state_split = sem("rowmax"), sem("exps"), sem("recip_ready"), sem("state_sum"), sem("state_hi"), sem("state_split")
        attn_hi, sums_ready, probs3_ready, stored = sem("attn_hi"), sem("sums_ready"), sem("probs3_ready"), sem("stored")
        result_free = sem("result_free")

        x_g = x.rearrange("(g p h) c d -> g (h c) p d", p=NP, h=2)
        c_g = ctx_in.rearrange("(g p h) c d -> g (h c) p d", p=NP, h=2)
        y_g = out.rearrange("(g q p h) c d -> g q (h c) p d", q=2, p=2, h=2)
        m_g = mask.rearrange("(g k) s -> g (k s)", k=GB)

        blk = stack.enter_context(nc.Block())

        def w_in(m):
            return m.rearrange("(k p) h -> p k h", p=P)

        @blk.sync
        def _(sp):
            def hold(signal, n):
                sp.wait_ge(signal, n)
                sp.sem_inc(sp_held, 1)

            def load_group(g):
                sp.dma_start(x_raw[:], x_g[g]).then_inc(group_loaded, 16)
                sp.dma_start(c_raw[:], c_g[g]).then_inc(group_loaded, 16)
                sp.dma_start(mrow_u8[:].rearrange("r p k -> r (p k)"),
                             m_g[g].unsqueeze(0).broadcast_to([P, TOK])).then_inc(group_loaded, 16)

            def iteration(g, last):
                if not last:
                    for i in range(2):
                        hold(proj_full[i], g * (p_n // 2) + P_BASE)
                    hold(normed, g + 1)
                    hold(mix_ready, g + 1)
                    load_group(g + 1)
                for q in range(2):
                    i, n = p_count(g, ("P", "PV", q), last)
                    hold(proj_free[i], n)
                    sp.dma_start(y_g[g, q], result[:, 2 * q:2 * q + 2, :]).then_inc(stored, 16)
                sp.wait_ge(stored, 32 * g + 32)
                sp.sem_inc(result_free, 1)

            sp.dma_start(ident[:], cst_ident).then_inc(const_loaded, 16)
            sp.dma_start(block[:], cst_block).then_inc(const_loaded, 16)
            sp.dma_start(parity[:], cst_parity).then_inc(const_loaded, 16)
            sp.dma_start(own_slot[:], cst_own_slot).then_inc(const_loaded, 16)
            sp.dma_start(mask_u8[:], mask.rearrange("(p h) s -> p (h s)", h=2)).then_inc(mask_loaded, 16)
            sp.wait_ge(w0_cleared, 1)
            for i, n in enumerate(("Wn", "Wm", "Wo", "Wl")):
                for h in range(2):
                    sp.dma_start(w0_bd[C * h:C * h + C, i, C * h:C * h + C], w[f"L0_xattn_{n}"]).then_inc(w0_loaded, 16)
            for i, n in enumerate(("bn", "bm", "bl")):
                for h in range(2):
                    sp.dma_start(w0_cols[C * h:C * h + C, i:i + 1], w[f"L0_xattn_{n}"].unsqueeze(1)).then_inc(w0_loaded, 16)
            for h in range(2):
                sp.dma_start(bo_row[:, h, :], w["L0_xattn_bo"].unsqueeze(0).broadcast_to([P, C])).then_inc(w0_loaded, 16)
            sp.sem_inc(result_free, 1)
            load_group(0)
            with sp.Fori(0, NG - 1) as g:
                iteration(g, False)
            iteration(NG - 1, True)

        @blk.tensor
        def _(pe):
            def split_product(o, lhs, rhs, first, last):
                (lh, ll), (rh, rl) = lhs, rhs
                pe.matmul(o, lh, rh, start=first, stop=False)
                pe.matmul(o, lh, rl, start=False, stop=False)
                return pe.matmul(o, ll, rh, start=False, stop=last)

            def cut(hl, *index):
                return hl[0][index], hl[1][index]

            ALL = slice(None)

            def features_by_tokens(o, wname, m, operand):
                for k in range(NK):
                    mm_ = split_product(o, cut(wT[wname], ALL, k, slice(P * m, P * m + P)), cut(operand, ALL, k, ALL),
                                        k == 0, k == NK - 1)
                return mm_

            def half_group(o, wname, operand):
                for m in range(NK):
                    mm_ = features_by_tokens(o[:, HALF * m:HALF * m + HALF], wname, m, operand)
                return mm_

            def tokens_by_features(o, operand, wname, p):
                for k in range(NK):
                    mm_ = split_product(o, cut(operand, ALL, k, slice(P * p, P * p + P)), cut(wT[wname], ALL, k, ALL),
                                        k == 0, k == NK - 1)
                return mm_

            def wait_copied(g, last, steps, filling=None):
                base = 0 if g is None else g * (p_n // 2)
                need = {}
                for step in steps:
                    bk, n = p_count(None if g is None else 0, step, last)
                    need[bk] = max(need.get(bk, 0), n)
                if filling:
                    bk, n = p_count(None if g is None else 0, filling, last)
                    need[bk] = max(need.get(bk, 0), n - 1)
                for bk, n in need.items():
                    if n:
                        pe.wait_ge(proj_free[bk], base + n)

            def proj_step(g, step, last):
                _, name, i = step
                bk, n = p_count(g, step, last)
                o = proj[bk]
                wait_copied(g, last, [("P", "AT" + name[1], i)] if name in ("O1", "O2") else [], filling=step)
                if name == "xT":
                    if i == 0 and g is None:
                        pe.wait_ge(group_loaded, 48)
                    elif i == 0:
                        pe.wait_ge(group_loaded, g * 48 + 96)
                    for p in range(NP):
                        mm_ = pe.transpose(o[:, P * p:P * p + P], x_raw[:, p, P * i:P * i + P], ident[:])
                elif name == "cT":
                    for p in range(NP):
                        mm_ = pe.transpose(o[:, P * p:P * p + P], c_raw[:, p, P * i:P * i + P], ident[:])
                elif name == "nT":
                    if i == 0:
                        pe.wait_ge(normed, 1 if g is None else g + 2)
                        pe.wait_ge(mix_ready, 1 if g is None else g + 2)
                    for p in range(NP):
                        mm_ = pe.matmul(o[:, P * p:P * p + P], c_norm[:, p, P * i:P * i + P], mix[:, p, :],
                                        start=True, stop=True)
                elif name in ("Mn", "Mm"):
                    src, wi = (x_norm, 0) if name == "Mn" else (c_norm, 1)
                    for q in range(2):
                        mm_ = pe.matmul(o[:, D * q:D * q + D], w0T[:, wi, :], src[:, 2 * i + q, :], start=True, stop=True)
                elif name == "V0":
                    for q in range(2):
                        for s in range(2):
                            mm_ = pe.matmul(o[:, (2 * q + s) * P:(2 * q + s + 1) * P], c_raw[:, 2 * i + q, P * s:P * s + P],
                                            wv0[:], start=True, stop=True)
                elif name in ("K1", "K2", "K3"):
                    l = int(name[1])
                    mm_ = features_by_tokens(o[:], f"k{l}", i, nT if l < 3 else cT)
                elif name in ("V1", "V2", "V3"):
                    l = int(name[1])
                    for q in range(2):
                        mm_ = tokens_by_features(o[:, D * q:D * q + D], nT if l < 3 else cT, f"v{l}", 2 * i + q)
                elif name in ("Q1", "Q2"):
                    l = int(name[1])
                    pe.wait_ge(state_split, 4 * g + (2 * l - 1 + i))
                    mm_ = half_group(o, f"q{l}", state_hl)
                elif name in ("AT1", "AT2"):
                    for q in range(2):
                        p = 2 * i + q
                        for c in range(2):
                            ba, _, na = ring_count(g, a_at[("A", int(name[2]), p)] + c, a_n)
                            pe.wait_ge(weighted_free[ba], na)
                        for h in range(2):
                            mm_ = pe.transpose(o[:, (2 * q + h) * P:(2 * q + h + 1) * P],
                                               attn[:, p, h].rearrange("t j d -> t (j d)"), ident[:])
                elif name in ("O1", "O2"):
                    mm_ = half_group(o, f"o{name[1]}", attnT)
                elif name == "XN":
                    for q in range(2):
                        p = 2 * i + q
                        for k in range(NK):
                            mm_ = pe.transpose(o[:, D * q + P * k:D * q + P * k + P], state[:, k, P * p:P * p + P], ident[:])
                elif name == "PV":
                    bt, _, nt = ring_count(g, t_at[("T", 3, i)], t_n)
                    pe.wait_ge(turned_free[bt], nt)
                    for q in range(2):
                        p = 2 * i + q
                        mm_ = pe.matmul(o[:, D * q:D * q + D], probsT[:, i, P * q:P * q + P], v3[:, p, :], start=True, stop=True)
                mm_.then_inc(proj_full[bk], 1)

            def weight_step(step):
                name = step[1]
                bk, n = p_count(None, step, False)
                o = proj[bk]
                wait_copied(None, False, {"W0": [("P", "W0T", 0)], "VW3": [("P", "Wo3T", 0)]}.get(name, []), filling=step)
                if name == "W0T":
                    pe.wait_ge(const_loaded, 64)
                    pe.wait_ge(w0_loaded, 16 * 16)
                    pe.wait_ge(mask_ready, 1)
                    for i in range(3):
                        pe.transpose(o[:, P * i:P * i + P], w0_bd[:, i, :], ident[:])
                    mm_ = pe.transpose(o[:, 3 * P:3 * P + B // 2], mask_f[:], ident[0:B // 2, 0:B // 2])
                elif name == "W0":
                    pe.wait_ge(bl_ready, 1)
                    pe.matmul(o[:, 0:P], bl_wide, w0T[:, 2, :], start=True, stop=True)
                    mm_ = pe.matmul(o[:, P:2 * P], w0_bd[:, 3, :], w0T[:, 2, :], start=True, stop=True)
                elif name == "MS":
                    mm_ = pe.matmul(o[:, 0:B // 2], block[:], mask_col[:], start=True, stop=True)
                elif name == "Wo3T":
                    pe.wait_ge(w3_loaded, 64)
                    for k in range(NK):
                        for m in range(NK):
                            mm_ = pe.transpose(o[:, D * k + P * m:D * k + P * m + P], raw["o3"][:, m, P * k:P * k + P], ident[:])
                elif name == "M3":
                    for k in range(NK):
                        for m in range(NK):
                            mm_ = pe.matmul(o[:, D * k:D * k + D], raw["k3"][:, m, P * k:P * k + P], raw["q3"][:, m, :],
                                            start=m == 0, stop=m == NK - 1)
                elif name == "VW3":
                    for k in range(NK):
                        for m in range(NK):
                            mm_ = pe.matmul(o[:, D * k:D * k + D], raw["v3"][:, m, P * k:P * k + P], wo3T[:, m, :],
                                            start=m == 0, stop=m == NK - 1)
                elif name in ("VB1", "VB2"):
                    l = int(name[2])
                    pe.wait_ge(bias_step, 5 * l)
                    for m in range(NK):
                        mm_ = pe.transpose(o[:, P * m:P * m + P], v_bias_wide[:, l - 1, m, :], ident[:])
                else:
                    which, l = name[1], name[2]
                    if which == "q":
                        pe.wait_ge(w1_loaded if l == "1" else w2_loaded, 64)
                    src = raw[which + l] if which != "o" else o_sorted[int(l) - 1]
                    if which == "o":
                        pe.wait_ge(o_sorted_ready, int(l))
                    for k in range(NK):
                        for m in range(NK):
                            mm_ = pe.transpose(o[:, D * k + P * m:D * k + P * m + P], src[:, m, P * k:P * k + P], ident[:])
                mm_.then_inc(proj_full[bk], 1)

            def scores_step(g, step, last):
                _, l, i = step
                bk, n, _ = ring_count(g, s_at[step], s_n)
                o = scores[bk]
                pe.wait_ge(scores_free[bk], n)
                if l == 0:
                    if i == 0:
                        for r in range(2):
                            pe.wait_ge(proj_free[r], g * (p_n // 2) + (P_BASE - 1))
                    h = C * (i % 2)
                    for u in range(2):
                        mm_ = pe.matmul(o[:, D * u:D * u + D], mn[h:h + C, i // 2, P * u:P * u + P], mm[h:h + C, i // 2, :],
                                        start=True, stop=True)
                elif l < 3:
                    if i == 0:
                        pe.wait_ge(k_spread, 4 * g + (2 + 2 * l))
                    if i % 4 == 0:
                        wait_copied(g, last, [("P", f"Q{l}", i // 4)])
                    for c in range(NK):
                        mm_ = pe.matmul(o[:, D * c:D * c + D], qe[:, c, i].rearrange("p q t -> p (q t)"),
                                        kbd[l - 1][:, c, i].rearrange("p r s -> p (r s)"), start=True, stop=True)
                else:
                    wait_copied(g, last, [("P", "O2", i), ("P", "K3", 0), ("P", "K3", 1)])
                    for q in range(2):
                        p = 2 * i + q
                        for k in range(NK):
                            mm_ = pe.matmul(o[:, P * q:P * q + P], state[:, k, P * p:P * p + P], k3T[:, k, P * p:P * p + P],
                                            start=k == 0, stop=k == NK - 1)
                mm_.then_inc(scores_full[bk], 1)

            def turn_step(g, step):
                _, l, i = step
                for c in range(2 if l in (1, 2) else 1):
                    bk, n, _ = ring_count(g, t_at[step] + c, t_n)
                    o = turned[bk]
                    pe.wait_ge(turned_free[bk], n)
                    if l == 0:
                        ba, _, na = ring_count(g, s_at[("S", 0, i)], s_n)
                        pe.wait_ge(scores_free[ba], na)
                        for s in range(2):
                            for u in range(2):
                                mm_ = pe.transpose(o[:, D * s + P * u:D * s + P * u + P],
                                                   probs[:, i % 4, D * u + P * s:D * u + P * s + P], ident[:])
                    elif l < 3:
                        if c == 0:
                            pe.wait_ge(exps, 18 * g + (8 * (l - 1) + 2 * i + 2))
                        e = probs[:, 2 * (i % 2):2 * (i % 2) + 2, :].rearrange("t a (j k) -> t (a j) k", k=P)
                        for j in range(4):
                            mm_ = pe.transpose(o[:, P * j:P * j + P], e[:, 4 * c + j, :], ident[:])
                    else:
                        pe.wait_ge(probs3_ready, 2 * g + (i + 1))
                        for q in range(2):
                            mm_ = pe.transpose(o[:, P * q:P * q + P], probs3[:, 2 * i + q].rearrange("t b s -> t (b s)"), ident[:])
                    mm_.then_inc(turned_full[bk], 1)

            def weighted_step(g, step, last):
                _, l, i = step
                for c in range(2 if l in (1, 2) else 1):
                    n0 = a_at[step] + c
                    bk, n, _ = ring_count(g, n0, a_n)
                    o = weighted[bk]
                    if l or i % 2 == 0:
                        pe.wait_ge(weighted_free[bk], n)
                    bt, _, nt = ring_count(g, t_at[("T", l, i)] + c, t_n)
                    pe.wait_ge(turned_free[bt], nt)
                    if l == 0:
                        if i == 0:
                            for r in range(2):
                                pe.wait_ge(proj_free[r], g * (p_n // 2) + P_BASE)
                        for u in range(2):
                            for s in range(2):
                                mm_ = pe.matmul(o[:, (2 * (i % 2) + u) * V0W:(2 * (i % 2) + u + 1) * V0W],
                                                probsT[:, i % 4, D * s + P * u:D * s + P * u + P], v0[:, i, s, :],
                                                start=s == 0, stop=s == 1)
                    else:
                        if l == 1 and i == 0 and c == 0:
                            pe.wait_ge(sum_columns_ready, g + 1)
                        if i % 2 == 0 and c == 0:
                            wait_copied(g, last, [("P", f"V{l}", i // 2)])
                        e = probsT[:, 2 * (i % 2) + c, :].rearrange("k (j t) -> k j t", t=P)
                        for j in range(4):
                            mm_ = pe.matmul(o[:, 2 * VW * j:2 * VW * (j + 1)], e[:, j, :],
                                            v2[l - 1][:, i, 4 * c + j].rearrange("k b v -> k (b v)"), start=True, stop=True)
                    if l or i % 2:
                        mm_.then_inc(weighted_full[bk], 1)

            def iteration(g, last):
                for step in (LAST_ORDER if last else ORDER):
                    if step[0] == "P":
                        proj_step(g, step, last)
                    elif step[0] == "S":
                        scores_step(g, step, last)
                    elif step[0] == "T":
                        turn_step(g, step)
                    elif step[0] == "A":
                        weighted_step(g, step, last)

            for free in scores_free + turned_free + weighted_free:
                pe.sem_inc(free, 1)
            pe.wait_ge(cleared, 1)
            for step in WEIGHT_STEPS:
                weight_step(step)
            for step in front_order():
                proj_step(None, step, False)
            with pe.Fori(0, NG - 1) as g:
                iteration(g, False)
            iteration(NG - 1, True)

        @blk.scalar
        def _(act):
            def full(g, step, last):
                bk, n = p_count(g, step, last)
                act.wait_ge(proj_full[bk], n)
                return proj[bk], proj_free[bk]

            def proj_step(g, step, last):
                _, name, i = step
                if name == "xT":
                    o, free = full(g, step, last)
                    act.activation(xT[:, i, :], o[:], ACT.Copy).then_inc(free, 1)
                elif name in ("cT", "nT"):
                    o, _ = full(g, step, last)
                    act.activation((cT if name == "cT" else nT)[0][:, i, :], o[:], ACT.Copy).then_inc(ctx_hi, 1)
                elif name in ("Mn", "Mm"):
                    o, free = full(g, step, last)
                    dst, col = (mn, 0) if name == "Mn" else (mm, 1)
                    act.activation(dst[:, 2 * i:2 * i + 2, :], o[:].rearrange("c (q t) -> c q t", q=2), ACT.Identity,
                                   bias=w0_cols[:, col:col + 1]).then_inc(free, 1)
                elif name in ("K1", "K2"):
                    o, free = full(g, step, last)
                    l = int(name[1])
                    act.wait_ge(k_spread, 4 * g + (2 * l - 1 + i))
                    act.activation(k_tmp[:, i, :], o[:], ACT.Identity, bias=k_bias[:, l - 1, i:i + 1]).then_inc(free, 1)
                elif name in ("V1", "V2"):
                    o, free = full(g, step, last)
                    act.sem_inc(act_held, 1)
                    for q in range(2):
                        for h in range(2):
                            rows = slice(C * h, C * h + C)
                            ins = act.activation(v2[int(name[1]) - 1][rows, 2 * i + q, :, h, 0:VW - 1],
                                                 o[rows, D * q:D * q + D].rearrange("k (j v) -> k j v", j=NJ), ACT.Copy,
                                                 scale=mask_col[rows, bass.ds(NP * g + (2 * i + q), 1)])
                    ins.then_inc(free, 1)
                elif name == "K3":
                    o, free = full(g, step, last)
                    act.activation(k3T[:, i, :], o[:], ACT.Copy).then_inc(free, 1)
                elif name == "V3":
                    o, free = full(g, step, last)
                    act.activation(v3[:, 2 * i:2 * i + 2, :], o[:].rearrange("s (q h) -> s q h", q=2), ACT.Copy).then_inc(free, 1)
                elif name in ("Q1", "Q2"):
                    o, free = full(g, step, last)
                    for q in range(2):
                        ins = act.activation(qe[:, :, 4 * i:4 * i + 4, q, :], o[:].rearrange("p (k b t) -> p k b t", k=NK, t=C),
                                             ACT.Identity, scale=parity[:, q:q + 1])
                    ins.then_inc(free, 1)
                elif name in ("AT1", "AT2"):
                    o, _ = full(g, step, last)
                    act.activation(attnT[0][:].rearrange("f q (b t) -> f q b t", t=C),
                                   o[:].rearrange("f (b q t) -> f q b t", q=2, t=C), ACT.Copy).then_inc(attn_hi, 1)
                elif name == "XN":
                    o, free = full(g, step, last)
                    if i == 0:
                        act.wait_ge(result_free, g + 1)
                    act.activation(result[:, 2 * i:2 * i + 2, :], o[:].rearrange("s (q h) -> s q h", q=2), ACT.Copy).then_inc(free, 1)

            def exp_step(g, step):
                _, l, i = step
                bk, _, n = ring_count(g, s_at[("S", l, i)], s_n)
                if l == 0:
                    act.wait_ge(rowmax, 26 * g + (i + 1))
                    for u in range(2):
                        ins = act.activation(probs[:, i % 4, D * u:D * u + D], scores[bk][:, D * u:D * u + D], ACT.Exp,
                                             bias=negmax[:, i % 2, u:u + 1])
                    ins.then_inc(scores_free[bk], 1)
                elif l < 3:
                    act.wait_ge(scores_free[bk], n)
                    e = probs[:, 2 * (i // 2 % 2):2 * (i // 2 % 2) + 2, :].rearrange("t a (j h s) -> t (a j) h s", h=2, s=C)
                    act.activation(e[:, :, i % 2, :], shifted[:, i % 2, :].rearrange("t (j s) -> t j s", s=C),
                                   ACT.Exp).then_inc(exps, 1)
                else:
                    act.wait_ge(scores_free[bk], n)
                    act.activation(probs[:, i, 0:P], shifted[:, i, 0:P], ACT.Exp).then_inc(exps, 1)

            def turn_step(g, step):
                _, l, i = step
                for c in range(2 if l in (1, 2) else 1):
                    bk, n, _ = ring_count(g, t_at[step] + c, t_n)
                    act.wait_ge(turned_full[bk], n)
                    slot = i % 4 if l == 0 else 2 * (i % 2) + c if l < 3 else i
                    width = 512 if l < 3 else D
                    act.activation(probsT[:, slot, 0:width], turned[bk][:, 0:width], ACT.Copy).then_inc(turned_free[bk], 1)

            def weight_step(step):
                name = step[1]
                if name in ("W0T", "W0", "MS", "VB1", "VB2"):
                    return
                o, free = full(None, step, False)
                v = o[:].rearrange("h (k m) -> h k m", k=NK)
                if name == "Wo3T":
                    act.wait_ge(const_loaded, 64)
                    act.activation(wo3T, v, ACT.Identity, scale=gates[:, 2:3]).then_inc(free, 1)
                elif name == "M3":
                    act.activation(wT["k3"][0][:], v, ACT.Copy, scale=D ** -0.5).then_inc(w_hi, 1)
                elif name == "VW3":
                    act.activation(wT["v3"][0][:], v, ACT.Copy).then_inc(w_hi, 1)
                else:
                    which, l = name[1], int(name[2])
                    if which == "o":
                        act.activation(wT[which + name[2]][0][:], v, ACT.Identity, scale=tgates[:, l - 1:l]).then_inc(w_hi, 1)
                    elif which == "q":
                        act.activation(wT[which + name[2]][0][:], v, ACT.Copy).then_inc(w_hi, 1)
                    else:
                        for k in range(NK):
                            ins = act.activation(wT[which + name[2]][0][:, k, :], v[:, k, :], ACT.Identity,
                                                 scale=gamma[:, l - 1, k:k + 1])
                        ins.then_inc(w_hi, 1)

            def iteration(g, last):
                for step in (LAST_ORDER if last else ORDER):
                    if step[0] == "P":
                        proj_step(g, step, last)
                    elif step[0] == "X":
                        exp_step(g, step)
                    elif step[0] == "T":
                        turn_step(g, step)

            for l in (1, 2):
                for n in "qkvo":
                    act.dma_start(raw[n + str(l)][:], w_in(w[f"L{l}_xattn_W{n}"])).then_inc((w1_loaded, w2_loaded)[l - 1], 16)
            act.wait_ge(scales_loaded, 9 * 16)
            act.activation(tgates[:], gates[:, 0:2], ACT.Tanh).then_inc(tanh_ready, 1)
            act.wait_ge(tanh_ready, 1)
            for step in WEIGHT_STEPS:
                weight_step(step)
            for step in front_order():
                proj_step(None, step, False)
            with act.Fori(0, NG - 1) as g:
                iteration(g, False)
            iteration(NG - 1, True)

        @blk.vector
        def _(dve):
            def full(g, step, last):
                bk, n = p_count(g, step, last)
                dve.wait_ge(proj_full[bk], n)
                return proj[bk], proj_free[bk], n

            def split_state(g, h, nth):
                half = slice(HALF * h, HALF * h + HALF)
                dve.tensor_copy(state_hl[0][:], state[:, :, half]).then_inc(state_hi, 1)
                dve.wait_ge(state_hi, 4 * g + (nth + 1))
                dve.tensor_tensor(state_hl[1][:], state[:, :, half], state_hl[0][:].bitcast(F32),
                                  ALU.subtract).then_inc(state_split, 1)

            def proj_step(g, step, last):
                _, name, i = step
                if name == "V0":
                    o, free, _ = full(g, step, last)
                    for q in range(2):
                        b = 4 * i + 2 * q
                        ins = dve.tensor_tensor(v0[:, b:b + 2, :, 0:C].rearrange("k b s c -> k s b c"),
                                                o[:, D * q:D * q + D].rearrange("k (s b c) -> k s b c", s=2, b=2),
                                                v0_bias[:].unsqueeze(1).broadcast_to([P, 2, 2, C]), ALU.add)
                    ins.then_inc(free, 1)
                elif name in ("cT", "nT"):
                    o, free, _ = full(g, step, last)
                    hi, lo = cT if name == "cT" else nT
                    n = 2 * (name == "nT") + i + 1
                    dve.wait_ge(ctx_hi, n if g is None else 4 * g + (4 + n))
                    dve.tensor_tensor(lo[:, i, :], o[:], hi[:, i, :].bitcast(F32), ALU.subtract).then_inc(free, 1)
                elif name in ("AT1", "AT2"):
                    o, free, _ = full(g, step, last)
                    dve.wait_ge(attn_hi, 4 * g + (2 * int(name[2]) - 1 + i))
                    dve.tensor_tensor(attnT[1][:].rearrange("f q (b t) -> f q b t", t=C),
                                      o[:].rearrange("f (b q t) -> f q b t", q=2, t=C),
                                      attnT[0][:].bitcast(F32).rearrange("f q (b t) -> f q b t", t=C),
                                      ALU.subtract).then_inc(free, 1)
                elif name in ("O1", "O2"):
                    o, free, n = full(g, step, last)
                    l = int(name[1])
                    for k in range(NK):
                        half = state[:, k, HALF * i:HALF * i + HALF]
                        ins = dve.scalar_tensor_tensor(out=half, in0=o[:, HALF * k:HALF * k + HALF], scalar=o_bias[:, l - 1, k:k + 1],
                                                       in1=half, op0=ALU.add, op1=ALU.add)
                    ins.then_inc(free, 1)
                    if name == "O1":
                        dve.wait_ge(free, n)
                        split_state(g, i, 2 + i)
                elif name == "PV":
                    o, free, _ = full(g, step, last)
                    bx, nx = p_count(g, ("P", "XN", i), last)
                    dve.wait_ge(proj_free[bx], nx)
                    r = result[:, 2 * i:2 * i + 2, :]
                    dve.tensor_tensor(r, o[:].rearrange("s (q h) -> s q h", q=2), r, ALU.add).then_inc(free, 1)

            def scores_step(g, step):
                _, l, i = step
                bk, n, _ = ring_count(g, s_at[step], s_n)
                s = scores[bk]
                dve.wait_ge(scores_full[bk], n)
                if l == 0:
                    dve.tensor_reduce(negmax[:, i % 2, 0:2], s[:].rearrange("t (u k) -> t u k", u=2), AX_X, ALU.max,
                                      negate=True).then_inc(rowmax, 1)
                elif l < 3:
                    sv = s[:].rearrange("t (j k) -> t j k", k=C)
                    dve.tensor_reduce(negmax[:, i % 2, :], sv, AX_X, ALU.max, negate=True).then_inc(rowmax, 1)
                    if l == 2 or i >= 2:
                        dve.wait_ge(exps, 18 * g + (8 * (l - 1) + i - 1))
                    dve.wait_ge(rowmax, 26 * g + (8 * l + i + 1))
                    dve.tensor_tensor(shifted[:, i % 2, :].rearrange("t (j k) -> t j k", k=C), sv,
                                      negmax[:, i % 2, :].unsqueeze(2).broadcast_to([P, NJ, C]),
                                      ALU.add).then_inc(scores_free[bk], 1)
                else:
                    sv = s[:, 0:2 * P].rearrange("t (q h k) -> t q h k", q=2, h=2)
                    for h in range(2):
                        rows = slice(C * h, C * h + C)
                        ins = dve.tensor_reduce(negmax[rows, i, 0:2], sv[rows, :, h, :], AX_X, ALU.max, negate=True)
                    ins.then_inc(rowmax, 1)
                    dve.wait_ge(exps, 18 * g + (15 + i))
                    dve.wait_ge(rowmax, 26 * g + (25 + i))
                    for h in range(2):
                        rows = slice(C * h, C * h + C)
                        ins = dve.tensor_tensor(shifted[rows, i, 0:P].rearrange("t (q k) -> t q k", q=2), sv[rows, :, h, :],
                                                negmax[rows, i, 0:2].unsqueeze(2).broadcast_to([C, 2, C]), ALU.add)
                    ins.then_inc(scores_free[bk], 1)

            def normalise3(g, i):
                e = probs[:, i, 0:P].rearrange("t (q k) -> t q k", q=2)
                dve.wait_ge(exps, 18 * g + (17 + i))
                dve.reduce_sum(sums3[:, i, :], e, AX_X).then_inc(sums_ready, 1)
                dve.wait_ge(sums_ready, 2 * g + (i + 1))
                dve.reciprocal(recip3[:, i, :], sums3[:, i, :]).then_inc(recip_ready, 1)
                dve.wait_ge(recip_ready, 22 * g + (21 + i))
                for h in range(2):
                    rows = slice(C * h, C * h + C)
                    ins = dve.tensor_tensor(probs3[rows, 2 * i:2 * i + 2, h, :], e[rows],
                                            recip3[rows, i, :].unsqueeze(2).broadcast_to([C, 2, C]), ALU.mult)
                ins.then_inc(probs3_ready, 1)

            def weighted_step(g, step):
                _, l, i = step
                if l == 0:
                    if i % 2 == 0:
                        return
                    n0 = a_at[step]
                    bk, n, released = ring_count(g, n0, a_n)
                    p = i // 2
                    dve.wait_ge(weighted_full[bk], n)
                    sums = weighted[bk][:, 0:4 * V0W].rearrange("t (h u v) -> t h u v", h=2, u=2)
                    rz = recip[:, bk, 0:4].rearrange("t (h u) -> t h u", h=2)
                    dve.reciprocal(rz, sums[:, :, :, C]).then_inc(recip_ready, 1)
                    dve.wait_ge(recip_ready, 22 * g + (p + 1))
                    dve.tensor_tensor(x_scaled[:], sums[:, :, :, 0:C], rz.unsqueeze(3).broadcast_to([P, 2, 2, C]),
                                      ALU.mult).then_inc(weighted_free[bk], 1)
                    dve.wait_ge(weighted_free[bk], released)
                    toks = slice(P * p, P * p + P)
                    dve.tensor_tensor(state[:, :, toks].rearrange("f u (h c) -> f h u c", h=2), x_scaled[:],
                                      xT[:, :, toks].rearrange("f u (h c) -> f h u c", h=2), ALU.add).then_inc(state_sum, 1)
                    if p % 2:
                        dve.wait_ge(state_sum, 4 * g + (p + 1))
                        split_state(g, p // 2, p // 2)
                    return
                for c in range(2):
                    n0 = a_at[step] + c
                    bk, n, _ = ring_count(g, n0, a_n)
                    dve.wait_ge(weighted_full[bk], n)
                    sums = weighted[bk][:, 0:4 * 2 * VW].rearrange("t (j h v) -> t j h v", j=4, h=2)
                    rz = recip[:, bk, :].rearrange("t (j h) -> t j h", j=4)
                    dve.reciprocal(rz, sums[:, :, :, VW - 1]).then_inc(recip_ready, 1)
                    dve.wait_ge(recip_ready, 22 * g + (4 + 8 * (l - 1) + 2 * i + c + 1))
                    for q in range(2):
                        rows = slice(C * q, C * q + C)
                        ins = dve.tensor_tensor(attn[rows, i, :, 4 * c:4 * c + 4, :].rearrange("t h j d -> t j h d"),
                                                sums[rows, :, :, HD * q:HD * q + HD],
                                                rz[rows].unsqueeze(3).broadcast_to([C, 4, 2, HD]), ALU.mult)
                    ins.then_inc(weighted_free[bk], 1)

            def stats_step(g, p):
                if p == 0:
                    dve.wait_ge(group_loaded, 48 if g is None else 48 * g + 96)
                for t, src in ((p, x_raw), (NP + p, c_raw)):
                    ins = dve.bn_stats(stats[:, t, :], src[:, p, :])
                ins.then_inc(stats_ready, 1)

            def moments_step(g):
                dve.wait_ge(stats_ready, NP if g is None else NP * g + 2 * NP)
                dve.sem_inc(dve_held, 1)
                for t in range(2 * NP):
                    ins = dve.bn_aggr(mean_var[:, t, :], stats[:, t, :])
                ins.then_inc(mv_ready, 1)

            def sum_columns(g):
                for dst in v2:
                    for h in range(2):
                        rows = slice(C * h, C * h + C)
                        ins = dve.tensor_copy(dst[rows, :, :, h, VW - 1],
                                              mask_col[rows, bass.ds(NP * g, NP)].unsqueeze(2).broadcast_to([C, NP, NJ]))
                ins.then_inc(sum_columns_ready, 1)

            def weight_step(step):
                name = step[1]
                if name == "Wo3T":
                    return
                o, free, n = full(None, step, False)
                if name == "W0T":
                    dve.tensor_copy(mask_col[:], o[:, 3 * P:3 * P + B // 2])
                    dve.tensor_copy(w0T[:], o[:, 0:3 * P].rearrange("a (i b) -> a i b", i=3)).then_inc(free, 1)
                elif name == "W0":
                    dve.tensor_tensor(v0_bias[:], o[:, 0:P].rearrange("k (h c) -> k h c", h=2), bo_row, ALU.add)
                    dve.tensor_copy(wv0[:], o[:, P:2 * P]).then_inc(free, 1)
                elif name == "MS":
                    dve.tensor_scalar(mask_sum[:], o[:, 0:B // 2], 0.5, None, ALU.max).then_inc(free, 1)
                    dve.wait_ge(free, n)
                    dve.reciprocal(mix_col[:], mask_sum[:]).then_inc(mask_sum_ready, 1)
                    dve.wait_ge(mask_sum_ready, 1)
                    dve.tensor_tensor(mix_col[:], mix_col[:], mask_col[:], ALU.mult).then_inc(mix_col_ready, 1)
                    dve.wait_ge(mix_col_ready, 1)
                elif name in ("VB1", "VB2"):
                    l = int(name[2])
                    dve.tensor_tensor(bias_product[:], raw[f"o{l}"][:], o[:, 0:D].unsqueeze(1).broadcast_to([P, NK, D]),
                                      ALU.mult).then_inc(free, 1)
                    dve.wait_ge(free, n)
                    dve.reduce_sum(o_bias[:, l - 1, :], bias_product[:], AX_X).then_inc(o_bias_ready, 1)
                    dve.wait_ge(o_bias_ready, 2 * l - 1)
                    dve.tensor_scalar(o_bias[:, l - 1, :], o_bias[:, l - 1, :], tgates[:, l - 1:l], None,
                                      ALU.mult).then_inc(o_bias_ready, 1)
                else:
                    v = o[:].rearrange("h (k m) -> h k m", k=NK)
                    key = {"M3": "k3", "VW3": "v3"}.get(name, name[1:])
                    hi, lo = wT[key]
                    split = [s for s in WEIGHT_STEPS[4:] if s[1][:2] != "VB"]
                    dve.wait_ge(w_hi, split.index(step) + 1)
                    for k in range(NK):
                        if name[1] in "kv":
                            scalar = gamma[:, int(name[2]) - 1, k:k + 1]
                        else:
                            scalar = D ** -0.5 if name == "M3" else tgates[:, int(name[2]) - 1:int(name[2])] if name[1] == "o" else 1.0
                        ins = dve.scalar_tensor_tensor(out=lo[:, k, :], in0=v[:, k, :], scalar=scalar, in1=hi[:, k, :].bitcast(F32),
                                                       op0=ALU.mult, op1=ALU.subtract)
                    ins.then_inc(free, 1)

            def iteration(g, last):
                for step in (LAST_ORDER if last else ORDER):
                    if step[0] == "P":
                        proj_step(g, step, last)
                    elif step[0] == "S":
                        scores_step(g, step)
                    elif step[0] == "X" and step[1] == 3:
                        normalise3(g, step[2])
                    elif step[0] == "A":
                        weighted_step(g, step)
                    elif step[0] == "ST":
                        stats_step(g, step[1])
                    elif step[0] == "MV":
                        moments_step(g)
                    elif step[0] == "SC":
                        sum_columns(g)

            dve.wait_ge(mask_loaded, 16)
            dve.tensor_copy(mask_f[:], mask_u8[:]).then_inc(mask_ready, 1)
            dve.wait_ge(w0_loaded, 16 * 16)
            dve.tensor_copy(bl_wide, w0_cols[:, 2:3].broadcast_to([P, P])).then_inc(bl_ready, 1)
            dve.wait_ge(tanh_ready, 1)
            for step in WEIGHT_STEPS[:3]:
                weight_step(step)
            for p in range(NP):
                stats_step(None, p)
            moments_step(None)
            for l, loaded in ((1, w1_loaded), (2, w2_loaded)):
                dve.wait_ge(loaded, 64)
                for m in range(NK):
                    ins = dve.tensor_copy(o_sorted[l - 1][:, m, :].rearrange("o (q j d) -> o q j d", q=2, d=HD),
                                          raw[f"o{l}"][:, m, :].rearrange("o (j q d) -> o q j d", q=2, d=HD))
                ins.then_inc(o_sorted_ready, 1)
                for n, (name, bias) in enumerate((("k", k_bias), ("v", v_bias))):
                    dve.tensor_tensor(bias_product[:], raw[f"{name}{l}"][:], beta_row[:, l - 1, :].unsqueeze(1).broadcast_to([P, NK, D]),
                                      ALU.mult).then_inc(bias_step, 1)
                    dve.wait_ge(bias_step, 5 * (l - 1) + 2 * n + 1)
                    dve.reduce_sum(bias[:, l - 1, :], bias_product[:], AX_X).then_inc(bias_step, 1)
                    dve.wait_ge(bias_step, 5 * (l - 1) + 2 * n + 2)
                dve.tensor_copy(v_bias_wide[:, l - 1], v_bias[:, l - 1, :].unsqueeze(2).broadcast_to([P, NK, P])).then_inc(bias_step, 1)
            for step in WEIGHT_STEPS[3:]:
                weight_step(step)
            for step in front_order():
                proj_step(None, step, False)
            with dve.Fori(0, NG - 1) as g:
                iteration(g, False)
            iteration(NG - 1, True)

        @blk.gpsimd
        def _(pool):
            def hold(signal, n):
                pool.wait_ge(signal, n)
                pool.sem_inc(pool_held, 1)

            def spread_keys(g, l, last):
                for i in range(NK):
                    bk, n = p_count(g, ("P", f"K{l}", i), last)
                    pool.wait_ge(proj_free[bk], n)
                    each = [P, GB, 4, C]
                    pool.tensor_tensor(kbd[l - 1][:, i], k_tmp[:, i, :].rearrange("p (b s) -> p b s", s=C).unsqueeze(2).broadcast_to(each),
                                       own_slot[:].unsqueeze(1).unsqueeze(3).broadcast_to(each), ALU.mult).then_inc(k_spread, 1)

            def front(g):
                nth = 1 if g is None else g + 2
                hold(group_loaded, 48 * nth)
                pairs = slice(0, NP) if g is None else bass.ds(NP * g + NP, NP)
                each = [P, NP, P]
                if g is None:
                    hold(mix_col_ready, 1)
                pool.tensor_scalar(drop_row[:], mrow_u8[:], -1.0, 1.0, ALU.mult, ALU.add).then_inc(mix_step, 1)
                pool.tensor_tensor(mix[:], ident[:].unsqueeze(1).broadcast_to(each),
                                   mask_col[:, pairs].unsqueeze(2).broadcast_to(each), ALU.mult).then_inc(mix_step, 1)
                hold(mix_step, 4 * nth - 2)
                pool.tensor_tensor(drop_row[:], drop_row[:], mix_col[:, pairs].unsqueeze(2).broadcast_to(each),
                                   ALU.mult).then_inc(mix_step, 1)
                pool.wait_ge(mix_step, 4 * nth - 1)
                pool.tensor_tensor(drop_row[:], drop_row[:], block[:].unsqueeze(1).broadcast_to(each),
                                   ALU.mult).then_inc(mix_step, 1)
                pool.wait_ge(mix_step, 4 * nth)
                pool.tensor_tensor(mix[:], drop_row[:], mix[:], ALU.add).then_inc(mix_ready, 1)
                hold(mv_ready, nth)
                pool.tensor_scalar(var_eps[:], mean_var[:, :, 1], EPS, None, ALU.add).then_inc(ve_ready, 1)
                pool.wait_ge(ve_ready, nth)
                pool.tensor_tensor(rstd[:], var_eps[:], half_neg[:], ALU.pow).then_inc(rstd_ready, 1)
                hold(rstd_ready, nth)
                for t in list(range(NP, 2 * NP)) + list(range(NP)):
                    src, dst = (x_raw, x_norm) if t < NP else (c_raw, c_norm)
                    ins = pool.tensor_scalar(dst[:, t % NP, :], src[:, t % NP, :], mean_var[:, t, 0:1], rstd[:, t:t + 1],
                                             ALU.subtract, ALU.mult)
                ins.then_inc(normed, 1)

            pool.memset(w0_bd, 0.0).then_inc(w0_cleared, 1)
            for n in "qkvo":
                pool.dma_start(raw[n + "3"][:], w_in(w[f"L3_xattn_w_{n}"])).then_inc(w3_loaded, 16)
            for l in (1, 2):
                for k in range(NK):
                    half = slice(P * k, P * k + P)
                    pool.dma_start(gamma[:, l - 1, k:k + 1], w[f"L{l}_xattn_ln_gamma"][half].unsqueeze(1)).then_inc(scales_loaded, 16)
                pool.dma_start(beta_row[:, l - 1, :], w[f"L{l}_xattn_ln_beta"].unsqueeze(0).broadcast_to([P, D])).then_inc(scales_loaded, 16)
                pool.dma_start(gates[:, l - 1:l], w[f"L{l}_xattn_gate"].unsqueeze(0).broadcast_to([P, 1])).then_inc(scales_loaded, 16)
            pool.dma_start(gates[:, 2:3], w["L3_xattn_alpha"].unsqueeze(0).broadcast_to([P, 1])).then_inc(scales_loaded, 16)
            pool.memset(half_neg[:], -0.5)
            for t in (v2[0], v2[1], probs3):
                pool.memset(t[:], 0.0)
            pool.memset(v0[:, :, :, C], 1.0).then_inc(cleared, 1)
            pool.wait_ge(cleared, 1)
            front(None)
            pool.sem_inc(k_spread, 2)
            with pool.Fori(0, NG - 1) as g:
                spread_keys(g, 1, False)
                front(g)
                spread_keys(g, 2, False)
            for l in (1, 2):
                spread_keys(NG - 1, l, True)


_WEIGHTS = ['L0_xattn_Wn', 'L0_xattn_bn', 'L0_xattn_Wm', 'L0_xattn_bm', 'L0_xattn_Wl', 'L0_xattn_bl', 'L0_xattn_Wo',
            'L0_xattn_bo', 'L1_xattn_Wq', 'L1_xattn_Wk', 'L1_xattn_Wv', 'L1_xattn_Wo', 'L1_xattn_ln_gamma',
            'L1_xattn_ln_beta', 'L1_xattn_gate', 'L2_xattn_Wq', 'L2_xattn_Wk', 'L2_xattn_Wv', 'L2_xattn_Wo',
            'L2_xattn_ln_gamma', 'L2_xattn_ln_beta', 'L2_xattn_gate', 'L3_xattn_w_q', 'L3_xattn_w_k', 'L3_xattn_w_v',
            'L3_xattn_w_o', 'L3_xattn_alpha']


def kernel(**inputs):
    import numpy as _np
    import concourse.bacc as _bacc
    from concourse import mybir as _mybir
    from concourse.bass_utils import run_bass_kernel_spmd as _run

    nc = _bacc.Bacc("TRN2", target_bir_lowering=False, num_devices=1)
    arrays = {}

    def dram(name, a):
        a = _np.ascontiguousarray(a)
        arrays[f"in_{name}_dram"] = a
        return nc.dram_tensor(f"in_{name}_dram", a.shape, _mybir.dt.from_np(a.dtype), kind="ExternalInput").ap()

    x = dram("x", inputs["x"])
    ctx = dram("ctx_2048", inputs["ctx_2048"])
    mask = dram("mask", _np.asarray(inputs["mask_BxS2_bf1"]).view(_np.uint8))
    w = {n: dram(n, _np.asarray(inputs[n]).reshape(1) if _np.ndim(inputs[n]) == 0 else inputs[n]) for n in _WEIGHTS}
    rows = _np.arange(P)
    ident = dram("ident", _np.eye(P, dtype=_np.float32))
    block = dram("block", (rows[:, None] // C == rows[None, :] // C).astype(_np.float32))
    parity = dram("parity", ((rows[:, None] // HD % 2 == _np.arange(2)[None, :]) * HD ** -0.5).astype(_np.float32))
    own_slot = dram("own_slot", (rows[:, None] // 32 == _np.arange(4)[None, :]).astype(_np.float32))
    y = nc.dram_tensor("out_0_dram", (B, C, D), F32, kind="ExternalOutput").ap()
    build(nc, x, ctx, mask, w, ident, block, parity, own_slot, y)
    r = _run(nc, [arrays], core_ids=[0])
    return r.results[0]["out_0_dram"]
```

```python
from contextlib import ExitStack

import concourse.bass as bass
from concourse import mybir

F32 = mybir.dt.float32
F32R = mybir.dt.float32r
U8 = mybir.dt.uint8
ALU = mybir.AluOpType
ACT = mybir.ActivationFunctionType
AX_X = mybir.AxisListType.X

P = 128
B, C, D = 64, 64, 256
NH, HD = 16, 16
GB = 8
NG = B // GB
NP = GB // 2
TOK = GB * C
HALF = TOK // 2
NK = D // P
NJ = NH // 2
EPS = 1e-5
VW = HD * 2 + 1
V0W = C + 1


def group_order(front):
    def p(name, i):
        return [("P", name, i)]

    def at(kind, l, *i):
        return [(kind, l, n) for n in i]

    def S(l, i):
        return at("S", l, i)

    def X(l, i):
        return at("X", l, i)

    def T(l, i):
        return at("T", l, i)

    def A(l, i):
        return at("A", l, i)

    def nxt(step):
        return [step] if front else []

    def f(name, i):
        return nxt(("P", name, i))

    def copied(name, i):
        return [("E", name, i)]

    o = [("SC", 0)]
    o += S(0, 0) + S(0, 1) + X(0, 0) + p("K1", 0) + p("K1", 1)
    for b in range(2, GB):
        o += S(0, b) + X(0, b - 1) + {3: copied("K1", 0), 5: copied("K1", 1)}.get(b, [])
        o += T(0, b - 2) + (A(0, b - 3) if b > 2 else [])
        o += X(0, 7) if b == 7 else []
        o += nxt(("ST", b - 6)) if b > 5 else []
    o += T(0, 6) + A(0, 5) + p("Q1", 0) + p("V1", 0) + T(0, 7) + copied("V1", 0) + A(0, 6) + nxt(("ST", 2))
    o += S(1, 0) + S(1, 1) + X(1, 0) + p("V1", 1) + A(0, 7)
    o += nxt(("ST", 3)) + nxt(("MV", 0))
    o += S(1, 2) + X(1, 1) + p("K2", 0) + S(1, 3) + p("Q1", 1) + T(1, 0) + copied("Q1", 1) + X(1, 2) + p("K2", 1)
    o += A(1, 0) + S(1, 4) + X(1, 3) + S(1, 5) + T(1, 1) + X(1, 4)
    o += S(1, 6) + A(1, 1) + X(1, 5) + S(1, 7) + T(1, 2) + X(1, 6) + p("K3", 1) + p("AT1", 0)
    o += A(1, 2) + X(1, 7) + p("O1", 0) + T(1, 3) + p("K3", 0) + p("V2", 0) + p("Q2", 0)
    o += A(1, 3) + S(2, 0) + S(2, 1) + X(2, 0) + p("AT1", 1) + p("V2", 1)
    o += S(2, 2) + X(2, 1) + S(2, 3) + p("O1", 1) + T(2, 0) + X(2, 2)
    o += p("V3", 0) + f("V3", 1) + p("Q2", 1)
    o += A(2, 0) + X(2, 3) + S(2, 4) + S(2, 5) + T(2, 1) + X(2, 4)
    o += S(2, 6) + A(2, 1) + X(2, 5) + S(2, 7) + T(2, 2) + X(2, 6) + f("Mn", 0) + p("AT2", 0)
    o += A(2, 2) + X(2, 7) + T(2, 3) + p("O2", 0) + f("Mn", 1)
    if not front:
        o += A(2, 3) + S(3, 0) + p("AT2", 1) + X(3, 0) + p("V3", 1) + p("O2", 1) + p("XN", 0)
        return o + S(3, 1) + T(3, 0) + X(3, 1) + p("PV", 0) + p("XN", 1) + T(3, 1) + p("PV", 1)
    o += A(2, 3) + S(3, 0) + f("xT", 0) + f("xT", 1) + p("AT2", 1) + f("cT", 0) + f("cT", 1) + f("Mm", 0)
    o += p("O2", 1) + X(3, 0) + f("nT", 0) + f("Mm", 1) + p("XN", 0) + T(3, 0) + S(3, 1) + X(3, 1) + f("nT", 1)
    return o + p("PV", 0) + p("XN", 1) + f("V0", 0) + T(3, 1) + f("V0", 1) + p("PV", 1)


def front_order():
    return [("P", n, i) for n in ("xT", "cT", "nT", "Mn", "Mm", "V0") for i in range(2)]


def prologue_order():
    def p(*names):
        return [("P", n, 0) for n in names]

    f = front_order()
    o = p("W0T") + f[0:2] + [("ST", n) for n in range(NP)] + [("MV", 0)]
    o += p("MS") + f[2:4] + [("NM", 0)] + p("Wq1") + [("TG", 0)] + p("Wk1", "Wv1") + [("NM", 1)]
    o += p("Wq2", "Wk2", "Wv2", "Wo3T", "M3") + f[4:8] + p("Wo1", "W0", "Wo2") + [("KB", 1)] + p("VW3")
    return o + f[8:] + [("KB", 2)] + p("VB1", "VB2") + [("OB", 1), ("OB", 2)]


RING = {"xT": "A", "cT": "A", "nT": "A", "V0": "A"}


def build(nc, x, ctx_in, mask, w, cst, out):
    ORDER = group_order(True)
    LAST_ORDER = group_order(False)
    PROLOGUE = prologue_order()
    FRONT = front_order()
    SPLIT_NAMES = [f"W{n}{l}" for n in "qkvo" for l in (1, 2)] + ["M3", "VW3"]
    SPLIT_WEIGHTS = [s for s in PROLOGUE if s[1] in SPLIT_NAMES]

    def numbered(order, kind):
        n, at = 0, {}
        for s in order:
            if kind == "A" and s[0] == "A" and s[1] == 0:
                at[s] = n
                n += s[2] % 2
            elif (RING.get(s[1], "P") if s[0] == "P" else s[0]) == kind:
                per = {"T": {1: 2, 2: 2}, "A": {1: 2, 2: 2}}.get(kind, {}).get(s[1], 1)
                at[s] = n
                n += per
        return at, n

    p_at, p_n = numbered(ORDER, "P")
    p_at_last, _ = numbered(LAST_ORDER, "P")
    pro_steps = [s for s in PROLOGUE if s[0] == "P"]
    p_at_pro, p_n_pro = {s: n for n, s in enumerate(pro_steps)}, len(pro_steps)
    s_at, s_n = numbered(ORDER, "S")
    t_at, t_n = numbered(ORDER, "T")
    a_at, a_n = numbered(ORDER, "A")
    assert p_n % 2 == 0 and s_n % 2 == 0 and t_n % 2 == 0 and a_n % 2 == 0
    pro_bank = {s: (n + 2 - p_n_pro) % 8 for s, n in p_at_pro.items()}
    PRO_FILLS = [list(pro_bank.values()).count(i) for i in range(8)]
    P_BASE = PRO_FILLS[0]
    assert P_BASE == PRO_FILLS[1] > 1

    def p_count(g, step, last):
        if g is None:
            bank_of = pro_bank[step]
            return bank_of, sum(pro_bank[s] == bank_of and n <= p_at_pro[step] for s, n in p_at_pro.items())
        n = (p_at_last if last else p_at)[step]
        return n % 2, g * (p_n // 2) + (P_BASE + n // 2 + 1)

    def ring_count(g, n, total):
        fills = g * (total // 2) + (n // 2 + 1)
        return n % 2, fills, g * (total // 2) + (n // 2 + 2)

    with ExitStack() as stack:
        def sb(name, shape, dt=F32):
            return stack.enter_context(nc.sbuf_tensor(name, shape, dt))

        def pair_of(name, shape):
            return sb(name + "_hi", shape, F32R), sb(name + "_lo", shape, F32R)

        def sem(name):
            return stack.enter_context(nc.semaphore(name))

        def bank(name):
            return stack.enter_context(nc.psum_tensor(name, [P, 512], F32))

        const = sb("const", [P, 2 * P + 6])
        ident = const[:, 0:P]
        block = const[:, P:2 * P]
        parity = const[:, 2 * P:2 * P + 2]
        own_slot = const[:, 2 * P + 2:2 * P + 6]
        w0_cols = sb("w0_cols", [P, 3])
        w0T = sb("w0T", [P, 3, P])
        wv0 = sb("wv0", [P, P])
        v0_bias = sb("v0_bias", [P, 2, C])
        work = sb("work", [P, 12, NK * D])
        raw = {n: work[:, i, :].rearrange("o (k h) -> o k h", k=NK)
               for i, n in enumerate(("q1", "k1", "v1", "q3", "q2", "k2", "v2", "k3", "o1", "v3", "o2", "o3"))}
        wT = {n: pair_of(f"wT_{n}", [P, NK, D]) for n in ("q1", "k1", "v1", "o1", "q2", "k2", "v2", "o2", "k3", "v3")}
        gamma = sb("gamma", [P, 2, NK])
        k_bias = sb("k_bias", [P, 2, NK])
        v_bias = sb("v_bias", [P, 2, NK])
        o_bias = sb("o_bias", [P, 2, NK])
        gates = sb("gates", [P, 3])
        tgates = sb("tgates", [P, 2])
        mask_u8 = sb("mask_u8", [B // 2, P], U8)
        mask_f = sb("mask_f", [B // 2, P])
        mask_col = sb("mask_col", [P, B // 2])
        mask_sum = sb("mask_sum", [P, B // 2])
        mix_col = sb("mix_col", [P, B // 2])
        half_neg = sb("half_neg", [P, 2 * NP])

        x_raw = sb("x_raw", [P, NP, D])
        c_raw = sb("c_raw", [P, NP, D])
        mrow_u8 = sb("mrow_u8", [P, NP, P], U8)
        stats = sb("stats", [P, 2 * NP, 6])
        mean_var = sb("mean_var", [P, 2 * NP, 2])
        var_eps = sb("var_eps", [P, 2 * NP])
        rstd = sb("rstd", [P, 2 * NP])
        x_norm = sb("x_norm", [P, NP, D])
        c_norm = sb("c_norm", [P, NP, D])
        drop_row = c_norm[:, 0:2, :].rearrange("r a (p k) -> r (a p) k", k=P)
        mix = sb("mix", [P, NP, P])
        xT = sb("xT", [P, NK, TOK])
        cT = pair_of("cT", [P, NK, TOK])
        nT = pair_of("nT", [P, NK, TOK])
        mn = pair_of("mn", [P, NP, D])
        mm = pair_of("mm", [P, NP, D])
        v0 = sb("v0", [P, GB, 2, V0W])
        state = sb("state", [P, NK, TOK])
        o_sorted = [state[:, l, :].rearrange("o (m h) -> o m h", m=NK) for l in range(2)]
        state_hl = pair_of("state", [P, NK, HALF])
        kbd = [sb(f"kbd{l}", [P, NK, GB, 4, C]) for l in (1, 2)]
        k_tmp = sb("k_tmp", [P, NK, TOK])
        w0_bd = kbd[0][:, 0, 0:2].rearrange("p a b c -> p (a b c)").rearrange("p (i b) -> p i b", i=4)
        kv_product = kbd[0][:, 1].rearrange("p a b c -> p (a b c)").rearrange("p (n m h) -> p n m h", n=4, m=NK)
        v_bias_row = [kv_product[:, 2 * l, 0, :] for l in range(2)]
        w0_raw = kbd[0][:, 0, 2].rearrange("p a b -> p (a b)").rearrange("p (i c) -> p i c", i=4)
        beta_row = kbd[1][:, 0, 0:2].rearrange("p a b c -> p (a b c)").rearrange("p (l h) -> p l h", l=2)
        v2 = [sb(f"v2_{l}", [P, NP, NJ, 2, VW]) for l in (1, 2)]
        qe = work[:, 8:12, :].rearrange("p a b -> p (a b)").rearrange("p (k b q t) -> p k b q t", k=NK, b=GB, q=2)
        negmax = sb("negmax", [P, 2, NJ])
        shifted = sb("shifted", [P, 2, 512])
        wo3T = shifted[:, :, 0:D]
        probs = work[:, 0:4, :]
        probsT = work[:, 4:8, :]
        recip = sb("recip", [P, 2, 8])
        x_scaled = sb("x_scaled", [P, 2, 2, C])
        attn = sb("attn", [P, NP, 2, NJ, HD])
        attnT = pair_of("attnT", [P, 2, HALF])
        k3T = sb("k3T", [P, NK, TOK])
        v3 = k_tmp[:].rearrange("p k t -> p (k t)").rearrange("p (q h) -> p q h", q=NP)
        sums3 = sb("sums3", [P, 2, 2])
        recip3 = sb("recip3", [P, 2, 2])
        probs3 = sb("probs3", [P, NP, 2, C])
        result = attn[:].rearrange("t p h j d -> t (p h j d)").rearrange("t (p h) -> t p h", p=NP)
        v_bias_wide = result[:, 2:4, :].rearrange("p l (m c) -> p l m c", m=NK)
        bl_wide, bo_row = result[:, 0, 0:P], result[:, 1, 0:C]

        scores = [bank("scores0"), bank("scores1")]
        turned = [bank("turned0"), bank("turned1")]
        weighted = [bank("weighted0"), bank("weighted1")]
        proj = [bank("proj0"), bank("proj1")] + scores + turned + weighted

        proj_full, proj_free = [sem(f"proj_full{i}") for i in range(8)], [sem(f"proj_free{i}") for i in range(8)]
        scores_full, scores_free = [sem(f"scores_full{i}") for i in range(2)], [sem(f"scores_free{i}") for i in range(2)]
        turned_full, turned_free = [sem(f"turned_full{i}") for i in range(2)], [sem(f"turned_free{i}") for i in range(2)]
        weighted_full = [sem(f"weighted_full{i}") for i in range(2)]
        weighted_free = [sem(f"weighted_free{i}") for i in range(2)]
        b0_loaded = sem("b0_loaded")
        w0_loaded, w3_loaded, w1_loaded, w2_loaded = sem("w0_loaded"), sem("w3_loaded"), sem("w1_loaded"), sem("w2_loaded")
        const_loaded, mask_loaded, scales_loaded = sem("const_loaded"), sem("mask_loaded"), sem("scales_loaded")
        group_loaded = sem("group_loaded")
        cleared, w0_ready = sem("cleared"), sem("w0_ready")
        mask_ready, mix_col_ready, mask_sum_ready = sem("mask_ready"), sem("mix_col_ready"), sem("mask_sum_ready")
        tanh_ready, bl_ready = sem("tanh_ready"), sem("bl_ready")
        pool_held, sp_held, dve_held, act_held = sem("pool_held"), sem("sp_held"), sem("dve_held"), sem("act_held")
        sum_columns_ready = sem("sum_columns_ready")
        w_hi, o_sorted_ready = sem("w_hi"), sem("o_sorted_ready")
        stats_ready, mv_ready = sem("stats_ready"), sem("mv_ready")
        ve_ready, rstd_ready, normed = sem("ve_ready"), sem("rstd_ready"), sem("normed")
        mix_step, mix_ready = sem("mix_step"), sem("mix_ready")
        half_ready = sem("half_ready")
        m_hi, ctx_hi, k_spread, kv_ready = sem("m_hi"), sem("ctx_hi"), sem("k_spread"), sem("kv_ready")
        bias_step, o_product_ready = sem("bias_step"), sem("o_product_ready")
        rowmax, exps, recip_ready = sem("rowmax"), sem("exps"), sem("recip_ready")
        state_sum, state_hi, state_split = sem("state_sum"), sem("state_hi"), sem("state_split")
        attn_hi, sums_ready, probs3_ready, stored = sem("attn_hi"), sem("sums_ready"), sem("probs3_ready"), sem("stored")
        result_free = sem("result_free")

        x_g = x.rearrange("(g p h) c d -> g (h c) p d", p=NP, h=2)
        c_g = ctx_in.rearrange("(g p h) c d -> g (h c) p d", p=NP, h=2)
        y_g = out.rearrange("(g q p h) c d -> g q (h c) p d", q=2, p=2, h=2)
        m_g = mask.rearrange("(g k) s -> g (k s)", k=GB)

        blk = stack.enter_context(nc.Block())

        def w_in(m):
            return m.rearrange("(k p) h -> p k h", p=P)

        @blk.sync
        def _(sp):
            def hold(signal, n):
                sp.wait_ge(signal, n)
                sp.sem_inc(sp_held, 1)

            def load_group(g):
                sp.dma_start(mrow_u8[:].rearrange("r p k -> r (p k)"),
                             m_g[g].unsqueeze(0).broadcast_to([P, TOK])).then_inc(group_loaded, 16)
                sp.dma_start(x_raw[:], x_g[g]).then_inc(group_loaded, 16)
                sp.dma_start(c_raw[:], c_g[g]).then_inc(group_loaded, 16)

            def iteration(g, last):
                if not last:
                    for i in range(2):
                        hold(proj_full[i], g * (p_n // 2) + P_BASE)
                    hold(normed, g + 1)
                    hold(mix_ready, g + 1)
                    load_group(g + 1)
                for q in range(2):
                    i, n = p_count(g, ("P", "PV", q), last)
                    hold(proj_free[i], n)
                    sp.dma_start(y_g[g, q], result[:, 2 * q:2 * q + 2, :]).then_inc(stored, 16)
                sp.wait_ge(stored, 32 * g + 32)
                sp.sem_inc(result_free, 1)

            sp.dma_start(const[:], cst).then_inc(const_loaded, 16)
            sp.dma_start(mask_u8[:], mask.rearrange("(p h) s -> p (h s)", h=2)).then_inc(mask_loaded, 16)
            load_group(0)
            for i, n in enumerate(("bn", "bm", "bl")):
                sp.dma_start(w0_cols[:, i:i + 1],
                             w[f"L0_xattn_{n}"].unsqueeze(1).unsqueeze(0).broadcast_to([2, C, 1])).then_inc(b0_loaded, 16)
            sp.dma_start(bo_row, w["L0_xattn_bo"].unsqueeze(0).broadcast_to([P, C])).then_inc(b0_loaded, 16)
            for n in "qkvo":
                sp.dma_start(raw[n + "2"][:], w_in(w[f"L2_xattn_W{n}"])).then_inc(w2_loaded, 16)
            for n in "qkvo":
                sp.dma_start(raw[n + "3"][:], w_in(w[f"L3_xattn_w_{n}"])).then_inc(w3_loaded, 16)
            sp.sem_inc(result_free, 1)
            for i in range(8):
                sp.wait_ge(proj_full[i], PRO_FILLS[i])
            with sp.Fori(0, NG - 1) as g:
                iteration(g, False)
            iteration(NG - 1, True)

        @blk.tensor
        def _(pe):
            def split_product(o, lhs, rhs, first, last):
                (lh, ll), (rh, rl) = lhs, rhs
                pe.matmul(o, lh, rh, start=first, stop=False)
                pe.matmul(o, lh, rl, start=False, stop=False)
                return pe.matmul(o, ll, rh, start=False, stop=last)

            def cut(hl, *index):
                return hl[0][index], hl[1][index]

            ALL = slice(None)

            def features_by_tokens(o, wname, m, operand):
                for k in range(NK):
                    mm_ = split_product(o, cut(wT[wname], ALL, k, slice(P * m, P * m + P)), cut(operand, ALL, k, ALL),
                                        k == 0, k == NK - 1)
                return mm_

            def half_group(o, wname, operand):
                for m in range(NK):
                    mm_ = features_by_tokens(o[:, HALF * m:HALF * m + HALF], wname, m, operand)
                return mm_

            def tokens_by_features(o, operand, wname, p):
                for k in range(NK):
                    mm_ = split_product(o, cut(operand, ALL, k, slice(P * p, P * p + P)), cut(wT[wname], ALL, k, ALL),
                                        k == 0, k == NK - 1)
                return mm_

            def wait_copied(g, last, steps, filling=None):
                base = 0 if g is None else g * (p_n // 2)
                need = {}
                for step in steps:
                    bk, n = p_count(None if g is None else 0, step, last)
                    need[bk] = max(need.get(bk, 0), n)
                if filling:
                    bk, n = p_count(None if g is None else 0, filling, last)
                    need[bk] = max(need.get(bk, 0), n - 1)
                for bk, n in need.items():
                    if n:
                        pe.wait_ge(proj_free[bk], base + n)

            def wait_front(name, g):
                for i in range(2):
                    step = ("P", name, i)
                    if name in RING:
                        bk, n, _ = ring_count(0, a_at[step], a_n)
                        n, per = n + 1 - a_n // 2, a_n // 2
                        if n > 0:
                            pe.wait_ge(weighted_free[bk], g * per + n)
                    else:
                        bk, n = p_count(0, step, False)
                        n, per = n - p_n // 2, p_n // 2
                        if n > 0:
                            pe.wait_ge(proj_free[bk], g * per + n)

            def proj_step(g, step, last):
                _, name, i = step
                if g is not None and name in RING:
                    bk, n, _ = ring_count(g, a_at[step], a_n)
                    o, signal = weighted[bk], weighted_full[bk]
                    pe.wait_ge(weighted_free[bk], n)
                else:
                    bk, n = p_count(g, step, last)
                    o, signal = proj[bk], proj_full[bk]
                used = [("P", "AT" + name[1], i)] if name in ("O1", "O2") else []
                if g is None and name in ("Mn", "Mm", "V0"):
                    used = [("P", "W0" if name == "V0" else "W0T", 0)]
                wait_copied(g, last, used, filling=None if g is not None and name in RING else step)
                if name == "xT":
                    if i == 0 and g is None:
                        pe.wait_ge(group_loaded, 48)
                    elif i == 0:
                        pe.wait_ge(group_loaded, g * 48 + 96)
                    for p in range(NP):
                        mm_ = pe.transpose(o[:, P * p:P * p + P], x_raw[:, p, P * i:P * i + P], ident)
                elif name == "cT":
                    for p in range(NP):
                        mm_ = pe.transpose(o[:, P * p:P * p + P], c_raw[:, p, P * i:P * i + P], ident)
                elif name == "nT":
                    if i == 0:
                        pe.wait_ge(normed, 1 if g is None else g + 2)
                        pe.wait_ge(mix_ready, 1 if g is None else g + 2)
                    for p in range(NP):
                        mm_ = pe.matmul(o[:, P * p:P * p + P], c_norm[:, p, P * i:P * i + P], mix[:, p, :],
                                        start=True, stop=True)
                elif name in ("Mn", "Mm"):
                    src, wi = (x_norm, 0) if name == "Mn" else (c_norm, 1)
                    for q in range(2):
                        mm_ = pe.matmul(o[:, D * q:D * q + D], w0T[:, wi, :], src[:, 2 * i + q, :], start=True, stop=True)
                elif name == "V0":
                    for q in range(2):
                        for s in range(2):
                            mm_ = pe.matmul(o[:, (2 * q + s) * P:(2 * q + s + 1) * P], c_raw[:, 2 * i + q, P * s:P * s + P],
                                            wv0[:], start=True, stop=True)
                elif name in ("K1", "K2", "K3"):
                    l = int(name[1])
                    if name == "K1" and i == 0:
                        wait_front("nT", g)
                    mm_ = features_by_tokens(o[:], f"k{l}", i, nT if l < 3 else cT)
                elif name in ("V1", "V2", "V3"):
                    l = int(name[1])
                    for q in range(2):
                        mm_ = tokens_by_features(o[:, D * q:D * q + D], nT if l < 3 else cT, f"v{l}", 2 * i + q)
                elif name in ("Q1", "Q2"):
                    l = int(name[1])
                    pe.wait_ge(state_split, 4 * g + (2 * l - 1 + i))
                    mm_ = half_group(o, f"q{l}", state_hl)
                elif name in ("AT1", "AT2"):
                    for q in range(2):
                        p = 2 * i + q
                        for c in range(2):
                            ba, _, na = ring_count(g, a_at[("A", int(name[2]), p)] + c, a_n)
                            pe.wait_ge(weighted_free[ba], na)
                        for h in range(2):
                            mm_ = pe.transpose(o[:, (2 * q + h) * P:(2 * q + h + 1) * P],
                                               attn[:, p, h].rearrange("t j d -> t (j d)"), ident)
                elif name in ("O1", "O2"):
                    mm_ = half_group(o, f"o{name[1]}", attnT)
                elif name == "XN":
                    for q in range(2):
                        p = 2 * i + q
                        for k in range(NK):
                            mm_ = pe.transpose(o[:, D * q + P * k:D * q + P * k + P], state[:, k, P * p:P * p + P], ident)
                elif name == "PV":
                    bt, _, nt = ring_count(g, t_at[("T", 3, i)], t_n)
                    pe.wait_ge(turned_free[bt], nt)
                    for q in range(2):
                        p = 2 * i + q
                        mm_ = pe.matmul(o[:, D * q:D * q + D], probsT[:, i, P * q:P * q + P], v3[:, p, :], start=True, stop=True)
                mm_.then_inc(signal, 1)

            def weight_step(step):
                name = step[1]
                bk, n = p_count(None, step, False)
                o = proj[bk]
                sources = {"W0": [("P", "W0T", 0)], "MS": [("P", "W0T", 0)], "VW3": [("P", "Wo3T", 0)]}
                wait_copied(None, False, sources.get(name, []), filling=step)
                if name == "W0T":
                    pe.wait_ge(const_loaded, 16)
                    pe.wait_ge(w0_ready, 2)
                    pe.wait_ge(mask_ready, 1)
                    for i in range(3):
                        pe.transpose(o[:, P * i:P * i + P], w0_bd[:, i, :], ident)
                    mm_ = pe.transpose(o[:, 3 * P:3 * P + B // 2], mask_f[:], ident[0:B // 2, 0:B // 2])
                elif name == "W0":
                    pe.wait_ge(bl_ready, 1)
                    pe.matmul(o[:, 0:P], bl_wide, w0T[:, 2, :], start=True, stop=True)
                    mm_ = pe.matmul(o[:, P:2 * P], w0_bd[:, 3, :], w0T[:, 2, :], start=True, stop=True)
                elif name == "MS":
                    mm_ = pe.matmul(o[:, 0:B // 2], block, mask_col[:], start=True, stop=True)
                elif name == "Wo3T":
                    pe.wait_ge(w3_loaded, 64)
                    for k in range(NK):
                        for m in range(NK):
                            mm_ = pe.transpose(o[:, D * k + P * m:D * k + P * m + P], raw["o3"][:, m, P * k:P * k + P], ident)
                elif name == "M3":
                    for k in range(NK):
                        for m in range(NK):
                            mm_ = pe.matmul(o[:, D * k:D * k + D], raw["k3"][:, m, P * k:P * k + P], raw["q3"][:, m, :],
                                            start=m == 0, stop=m == NK - 1)
                elif name == "VW3":
                    for k in range(NK):
                        for m in range(NK):
                            mm_ = pe.matmul(o[:, D * k:D * k + D], raw["v3"][:, m, P * k:P * k + P], wo3T[:, m, :],
                                            start=m == 0, stop=m == NK - 1)
                elif name in ("VB1", "VB2"):
                    l = int(name[2])
                    pe.wait_ge(bias_step, 2 * l)
                    for m in range(NK):
                        mm_ = pe.transpose(o[:, P * m:P * m + P], v_bias_wide[:, l - 1, m, :], ident)
                else:
                    which, l = name[1], name[2]
                    if which == "q":
                        pe.wait_ge(w1_loaded if l == "1" else w2_loaded, 64)
                    src = raw[which + l] if which != "o" else o_sorted[int(l) - 1]
                    if which == "o":
                        pe.wait_ge(o_sorted_ready, int(l))
                    for k in range(NK):
                        for m in range(NK):
                            mm_ = pe.transpose(o[:, D * k + P * m:D * k + P * m + P], src[:, m, P * k:P * k + P], ident)
                mm_.then_inc(proj_full[bk], 1)

            def scores_step(g, step, last):
                _, l, i = step
                bk, n, _ = ring_count(g, s_at[step], s_n)
                o = scores[bk]
                pe.wait_ge(scores_free[bk], n)
                if l == 0:
                    if i == 0:
                        wait_front("Mn", g)
                        wait_front("Mm", g)
                    h = C * (i % 2)
                    for u in range(2):
                        mm_ = split_product(o[:, D * u:D * u + D], cut(mn, slice(h, h + C), i // 2, slice(P * u, P * u + P)),
                                            cut(mm, slice(h, h + C), i // 2, ALL), True, True)
                elif l < 3:
                    if i == 0:
                        pe.wait_ge(k_spread, 4 * g + (2 + 2 * l))
                    if i % 4 == 0:
                        wait_copied(g, last, [("P", f"Q{l}", i // 4)])
                    for c in range(NK):
                        mm_ = pe.matmul(o[:, D * c:D * c + D], qe[:, c, i].rearrange("p q t -> p (q t)"),
                                        kbd[l - 1][:, c, i].rearrange("p r s -> p (r s)"), start=True, stop=True)
                else:
                    wait_copied(g, last, [("P", "O2", i), ("P", "K3", 0), ("P", "K3", 1)])
                    for q in range(2):
                        p = 2 * i + q
                        for k in range(NK):
                            mm_ = pe.matmul(o[:, P * q:P * q + P], state[:, k, P * p:P * p + P], k3T[:, k, P * p:P * p + P],
                                            start=k == 0, stop=k == NK - 1)
                mm_.then_inc(scores_full[bk], 1)

            def turn_step(g, step):
                _, l, i = step
                for c in range(2 if l in (1, 2) else 1):
                    bk, n, _ = ring_count(g, t_at[step] + c, t_n)
                    o = turned[bk]
                    pe.wait_ge(turned_free[bk], n)
                    if l == 0:
                        ba, _, na = ring_count(g, s_at[("S", 0, i)], s_n)
                        pe.wait_ge(scores_free[ba], na)
                        for s in range(2):
                            for u in range(2):
                                mm_ = pe.transpose(o[:, D * s + P * u:D * s + P * u + P],
                                                   probs[:, i % 4, D * u + P * s:D * u + P * s + P], ident)
                    elif l < 3:
                        if c == 0:
                            pe.wait_ge(exps, 18 * g + (8 * (l - 1) + 2 * i + 2))
                        e = probs[:, 2 * (i % 2):2 * (i % 2) + 2, :].rearrange("t a (j k) -> t (a j) k", k=P)
                        for j in range(4):
                            mm_ = pe.transpose(o[:, P * j:P * j + P], e[:, 4 * c + j, :], ident)
                    else:
                        pe.wait_ge(probs3_ready, 2 * g + (i + 1))
                        for q in range(2):
                            mm_ = pe.transpose(o[:, P * q:P * q + P], probs3[:, 2 * i + q].rearrange("t b s -> t (b s)"), ident)
                    mm_.then_inc(turned_full[bk], 1)

            def weighted_step(g, step, last):
                _, l, i = step
                for c in range(2 if l in (1, 2) else 1):
                    n0 = a_at[step] + c
                    bk, n, _ = ring_count(g, n0, a_n)
                    o = weighted[bk]
                    if l or i % 2 == 0:
                        pe.wait_ge(weighted_free[bk], n)
                    bt, _, nt = ring_count(g, t_at[("T", l, i)] + c, t_n)
                    pe.wait_ge(turned_free[bt], nt)
                    if l == 0:
                        if i == 0:
                            wait_front("V0", g)
                        for u in range(2):
                            for s in range(2):
                                mm_ = pe.matmul(o[:, (2 * (i % 2) + u) * V0W:(2 * (i % 2) + u + 1) * V0W],
                                                probsT[:, i % 4, D * s + P * u:D * s + P * u + P], v0[:, i, s, :],
                                                start=s == 0, stop=s == 1)
                    else:
                        if l == 1 and i == 0 and c == 0:
                            pe.wait_ge(sum_columns_ready, g + 1)
                        if i % 2 == 0 and c == 0:
                            wait_copied(g, last, [("P", f"V{l}", i // 2)])
                        e = probsT[:, 2 * (i % 2) + c, :].rearrange("k (j t) -> k j t", t=P)
                        for j in range(4):
                            mm_ = pe.matmul(o[:, 2 * VW * j:2 * VW * (j + 1)], e[:, j, :],
                                            v2[l - 1][:, i, 4 * c + j].rearrange("k b v -> k (b v)"), start=True, stop=True)
                    if l or i % 2:
                        mm_.then_inc(weighted_full[bk], 1)

            def iteration(g, last):
                for step in (LAST_ORDER if last else ORDER):
                    if step[0] == "P":
                        proj_step(g, step, last)
                    elif step[0] == "S":
                        scores_step(g, step, last)
                    elif step[0] == "T":
                        turn_step(g, step)
                    elif step[0] == "A":
                        weighted_step(g, step, last)

            for free in scores_free + turned_free + weighted_free:
                pe.sem_inc(free, 1)
            for step in PROLOGUE:
                if step in FRONT:
                    proj_step(None, step, False)
                elif step[0] == "P":
                    weight_step(step)
            for i in range(2, 8):
                pe.wait_ge(proj_free[i], PRO_FILLS[i])
            pe.wait_ge(cleared, 1)
            with pe.Fori(0, NG - 1) as g:
                iteration(g, False)
            iteration(NG - 1, True)

        @blk.scalar
        def _(act):
            def full(g, step, last):
                if g is not None and step[1] in RING:
                    bk, n, _ = ring_count(g, a_at[step], a_n)
                    act.wait_ge(weighted_full[bk], n)
                    return weighted[bk], weighted_free[bk]
                bk, n = p_count(g, step, last)
                act.wait_ge(proj_full[bk], n)
                return proj[bk], proj_free[bk]

            def proj_step(g, step, last):
                _, name, i = step
                if name == "xT":
                    o, free = full(g, step, last)
                    act.activation(xT[:, i, :], o[:], ACT.Copy).then_inc(free, 1)
                elif name in ("cT", "nT"):
                    o, _ = full(g, step, last)
                    act.activation((cT if name == "cT" else nT)[0][:, i, :], o[:], ACT.Copy).then_inc(ctx_hi, 1)
                elif name in ("Mn", "Mm"):
                    o, free = full(g, step, last)
                    if g is None:
                        act.wait_ge(b0_loaded, 64)
                    dst, col = (mn, 0) if name == "Mn" else (mm, 1)
                    act.activation(dst[0][:, 2 * i:2 * i + 2, :], o[:].rearrange("c (q t) -> c q t", q=2), ACT.Identity,
                                   bias=w0_cols[:, col:col + 1]).then_inc(m_hi, 1)
                elif name in ("K1", "K2"):
                    o, free = full(g, step, last)
                    l = int(name[1])
                    act.wait_ge(k_spread, 4 * g + (2 * l - 1 + i))
                    act.activation(k_tmp[:, i, :], o[:], ACT.Identity, bias=k_bias[:, l - 1, i:i + 1]).then_inc(free, 1)
                elif name in ("V1", "V2"):
                    o, free = full(g, step, last)
                    act.sem_inc(act_held, 1)
                    for q in range(2):
                        for h in range(2):
                            rows = slice(C * h, C * h + C)
                            ins = act.activation(v2[int(name[1]) - 1][rows, 2 * i + q, :, h, 0:VW - 1],
                                                 o[rows, D * q:D * q + D].rearrange("k (j v) -> k j v", j=NJ), ACT.Copy,
                                                 scale=mask_col[rows, bass.ds(NP * g + (2 * i + q), 1)])
                    ins.then_inc(free, 1)
                elif name == "K3":
                    o, free = full(g, step, last)
                    act.activation(k3T[:, i, :], o[:], ACT.Copy).then_inc(free, 1)
                elif name == "V3":
                    o, free = full(g, step, last)
                    act.activation(v3[:, 2 * i:2 * i + 2, :], o[:].rearrange("s (q h) -> s q h", q=2), ACT.Copy).then_inc(free, 1)
                elif name in ("Q1", "Q2"):
                    o, free = full(g, step, last)
                    for q in range(2):
                        ins = act.activation(qe[:, :, 4 * i:4 * i + 4, q, :], o[:].rearrange("p (k b t) -> p k b t", k=NK, t=C),
                                             ACT.Identity, scale=parity[:, q:q + 1])
                    ins.then_inc(free, 1)
                elif name in ("AT1", "AT2"):
                    o, _ = full(g, step, last)
                    act.activation(attnT[0][:].rearrange("f q (b t) -> f q b t", t=C),
                                   o[:].rearrange("f (b q t) -> f q b t", q=2, t=C), ACT.Copy).then_inc(attn_hi, 1)
                elif name == "XN":
                    o, free = full(g, step, last)
                    act.activation(result[:, 2 * i:2 * i + 2, :], o[:].rearrange("s (q h) -> s q h", q=2), ACT.Copy).then_inc(free, 1)

            def exp_step(g, step):
                _, l, i = step
                bk, _, n = ring_count(g, s_at[("S", l, i)], s_n)
                if l == 0:
                    act.wait_ge(rowmax, 26 * g + (i + 1))
                    for u in range(2):
                        ins = act.activation(probs[:, i % 4, D * u:D * u + D], scores[bk][:, D * u:D * u + D], ACT.Exp,
                                             bias=negmax[:, i % 2, u:u + 1])
                    ins.then_inc(scores_free[bk], 1)
                elif l < 3:
                    act.wait_ge(scores_free[bk], n)
                    e = probs[:, 2 * (i // 2 % 2):2 * (i // 2 % 2) + 2, :].rearrange("t a (j h s) -> t (a j) h s", h=2, s=C)
                    act.activation(e[:, :, i % 2, :], shifted[:, i % 2, :].rearrange("t (j s) -> t j s", s=C),
                                   ACT.Exp).then_inc(exps, 1)
                else:
                    act.wait_ge(scores_free[bk], n)
                    act.activation(probs[:, i, 0:P], shifted[:, i, 0:P], ACT.Exp).then_inc(exps, 1)

            def turn_step(g, step):
                _, l, i = step
                for c in range(2 if l in (1, 2) else 1):
                    bk, n, _ = ring_count(g, t_at[step] + c, t_n)
                    act.wait_ge(turned_full[bk], n)
                    slot = i % 4 if l == 0 else 2 * (i % 2) + c if l < 3 else i
                    width = 512 if l < 3 else D
                    act.activation(probsT[:, slot, 0:width], turned[bk][:, 0:width], ACT.Copy).then_inc(turned_free[bk], 1)

            def weight_step(step):
                name = step[1]
                if name in ("W0T", "W0", "MS"):
                    return
                o, free = full(None, step, False)
                v = o[:].rearrange("h (k m) -> h k m", k=NK)
                if name in ("VB1", "VB2"):
                    act.activation(v_bias_row[int(name[2]) - 1], o[:, 0:D], ACT.Copy).then_inc(free, 1)
                elif name == "Wo3T":
                    act.activation(wo3T, v, ACT.Identity, scale=gates[:, 2:3]).then_inc(free, 1)
                elif name == "M3":
                    act.activation(wT["k3"][0][:], v, ACT.Copy, scale=D ** -0.5).then_inc(w_hi, 1)
                elif name == "VW3":
                    act.activation(wT["v3"][0][:], v, ACT.Copy).then_inc(w_hi, 1)
                else:
                    which, l = name[1], int(name[2])
                    if which == "o":
                        act.activation(wT[which + name[2]][0][:], v, ACT.Identity, scale=tgates[:, l - 1:l]).then_inc(w_hi, 1)
                    elif which == "q":
                        act.activation(wT[which + name[2]][0][:], v, ACT.Copy).then_inc(w_hi, 1)
                    else:
                        for k in range(NK):
                            ins = act.activation(wT[which + name[2]][0][:, k, :], v[:, k, :], ACT.Identity,
                                                 scale=gamma[:, l - 1, k:k + 1])
                        ins.then_inc(w_hi, 1)

            def iteration(g, last):
                for step in (LAST_ORDER if last else ORDER):
                    if step[0] == "E" or step[0] == "P" and ("E",) + step[1:] not in ORDER:
                        proj_step(g, ("P",) + step[1:], last)
                    elif step[0] == "X":
                        exp_step(g, step)
                    elif step[0] == "T":
                        turn_step(g, step)

            def row_sum(terms, total, scale=1.0):
                return act.activation(terms, terms, ACT.Identity, scale=scale, accum_out=total)

            def bias_columns(l):
                for n, bias in ((2 * l - 2, k_bias), (2 * l - 1, v_bias)):
                    act.wait_ge(kv_ready, n + 1)
                    for m in range(NK):
                        ins = row_sum(kv_product[:, n, m, :], bias[:, l - 1, m:m + 1])
                ins.then_inc(bias_step, 1)
                act.wait_ge(bias_step, 2 * l - 1)
                act.activation(v_bias_wide[:, l - 1], v_bias[:, l - 1, :].unsqueeze(2).broadcast_to([P, NK, P]),
                               ACT.Copy).then_inc(bias_step, 1)

            for i, n in enumerate(("Wn", "Wm", "Wo", "Wl")):
                act.dma_start(w0_raw[:, i, :], w[f"L0_xattn_{n}"].unsqueeze(0).broadcast_to([2, C, C])).then_inc(w0_loaded, 16)
            for n in "qkvo":
                act.dma_start(raw[n + "1"][:], w_in(w[f"L1_xattn_W{n}"])).then_inc(w1_loaded, 16)
            for step in PROLOGUE:
                if step in FRONT:
                    proj_step(None, step, False)
                elif step[0] == "P":
                    weight_step(step)
                elif step[0] == "KB":
                    bias_columns(step[1])
                elif step[0] == "OB":
                    act.wait_ge(o_product_ready, step[1])
                    for m in range(NK):
                        row_sum(kv_product[:, 2 * step[1] - 1, m, :], o_bias[:, step[1] - 1, m:m + 1], tgates[:, step[1] - 1:step[1]])
                elif step[0] == "TG":
                    act.wait_ge(scales_loaded, 9 * 16)
                    act.activation(tgates[:], gates[:, 0:2], ACT.Tanh).then_inc(tanh_ready, 1)
                    act.wait_ge(tanh_ready, 1)
            with act.Fori(0, NG - 1) as g:
                iteration(g, False)
            iteration(NG - 1, True)

        @blk.vector
        def _(dve):
            def full(g, step, last):
                if g is not None and step[1] in RING:
                    bk, n, released = ring_count(g, a_at[step], a_n)
                    dve.wait_ge(weighted_full[bk], n)
                    return weighted[bk], weighted_free[bk], released
                bk, n = p_count(g, step, last)
                dve.wait_ge(proj_full[bk], n)
                return proj[bk], proj_free[bk], n

            def split_state(g, h, nth):
                half = slice(HALF * h, HALF * h + HALF)
                dve.tensor_copy(state_hl[0][:], state[:, :, half]).then_inc(state_hi, 1)
                dve.wait_ge(state_hi, 4 * g + (nth + 1))
                dve.tensor_tensor(state_hl[1][:], state[:, :, half], state_hl[0][:].bitcast(F32),
                                  ALU.subtract).then_inc(state_split, 1)

            def proj_step(g, step, last):
                _, name, i = step
                if name == "V0":
                    o, free, _ = full(g, step, last)
                    for q in range(2):
                        b = 4 * i + 2 * q
                        ins = dve.tensor_tensor(v0[:, b:b + 2, :, 0:C].rearrange("k b s c -> k s b c"),
                                                o[:, D * q:D * q + D].rearrange("k (s b c) -> k s b c", s=2, b=2),
                                                v0_bias[:].unsqueeze(1).broadcast_to([P, 2, 2, C]), ALU.add)
                    ins.then_inc(free, 1)
                elif name in ("cT", "nT"):
                    o, free, _ = full(g, step, last)
                    hi, lo = cT if name == "cT" else nT
                    n = 2 * (name == "nT") + i + 1
                    dve.wait_ge(ctx_hi, n if g is None else 4 * g + (4 + n))
                    dve.tensor_tensor(lo[:, i, :], o[:], hi[:, i, :].bitcast(F32), ALU.subtract).then_inc(free, 1)
                elif name in ("Mn", "Mm"):
                    o, free, _ = full(g, step, last)
                    (hi, lo), col = (mn, 0) if name == "Mn" else (mm, 1)
                    n = 2 * col + i + 1
                    dve.wait_ge(m_hi, n if g is None else 4 * g + (4 + n))
                    each = slice(2 * i, 2 * i + 2)
                    dve.scalar_tensor_tensor(out=lo[:, each, :], in0=o[:].rearrange("c (q t) -> c q t", q=2),
                                             scalar=w0_cols[:, col:col + 1], in1=hi[:, each, :].bitcast(F32), op0=ALU.add,
                                             op1=ALU.subtract).then_inc(free, 1)
                elif name in ("AT1", "AT2"):
                    o, free, _ = full(g, step, last)
                    dve.wait_ge(attn_hi, 4 * g + (2 * int(name[2]) - 1 + i))
                    dve.tensor_tensor(attnT[1][:].rearrange("f q (b t) -> f q b t", t=C),
                                      o[:].rearrange("f (b q t) -> f q b t", q=2, t=C),
                                      attnT[0][:].bitcast(F32).rearrange("f q (b t) -> f q b t", t=C),
                                      ALU.subtract).then_inc(free, 1)
                elif name in ("O1", "O2"):
                    o, free, n = full(g, step, last)
                    l = int(name[1])
                    for k in range(NK):
                        half = state[:, k, HALF * i:HALF * i + HALF]
                        ins = dve.scalar_tensor_tensor(out=half, in0=o[:, HALF * k:HALF * k + HALF], scalar=o_bias[:, l - 1, k:k + 1],
                                                       in1=half, op0=ALU.add, op1=ALU.add)
                    ins.then_inc(free, 1)
                    if name == "O1":
                        dve.wait_ge(free, n)
                        split_state(g, i, 2 + i)
                elif name == "PV":
                    o, free, _ = full(g, step, last)
                    bx, nx = p_count(g, ("P", "XN", i), last)
                    dve.wait_ge(proj_free[bx], nx)
                    r = result[:, 2 * i:2 * i + 2, :]
                    dve.tensor_tensor(r, o[:].rearrange("s (q h) -> s q h", q=2), r, ALU.add).then_inc(free, 1)

            def scores_step(g, step):
                _, l, i = step
                bk, n, _ = ring_count(g, s_at[step], s_n)
                s = scores[bk]
                dve.wait_ge(scores_full[bk], n)
                if l == 0:
                    dve.tensor_reduce(negmax[:, i % 2, 0:2], s[:].rearrange("t (u k) -> t u k", u=2), AX_X, ALU.max,
                                      negate=True).then_inc(rowmax, 1)
                elif l < 3:
                    sv = s[:].rearrange("t (j k) -> t j k", k=C)
                    dve.tensor_reduce(negmax[:, i % 2, :], sv, AX_X, ALU.max, negate=True).then_inc(rowmax, 1)
                    if l == 2 or i >= 2:
                        dve.wait_ge(exps, 18 * g + (8 * (l - 1) + i - 1))
                    dve.wait_ge(rowmax, 26 * g + (8 * l + i + 1))
                    dve.tensor_tensor(shifted[:, i % 2, :].rearrange("t (j k) -> t j k", k=C), sv,
                                      negmax[:, i % 2, :].unsqueeze(2).broadcast_to([P, NJ, C]),
                                      ALU.add).then_inc(scores_free[bk], 1)
                else:
                    sv = s[:, 0:2 * P].rearrange("t (q h k) -> t q h k", q=2, h=2)
                    for h in range(2):
                        rows = slice(C * h, C * h + C)
                        ins = dve.tensor_reduce(negmax[rows, i, 0:2], sv[rows, :, h, :], AX_X, ALU.max, negate=True)
                    ins.then_inc(rowmax, 1)
                    dve.wait_ge(exps, 18 * g + (15 + i))
                    dve.wait_ge(rowmax, 26 * g + (25 + i))
                    for h in range(2):
                        rows = slice(C * h, C * h + C)
                        ins = dve.tensor_tensor(shifted[rows, i, 0:P].rearrange("t (q k) -> t q k", q=2), sv[rows, :, h, :],
                                                negmax[rows, i, 0:2].unsqueeze(2).broadcast_to([C, 2, C]), ALU.add)
                    ins.then_inc(scores_free[bk], 1)

            def normalise3(g, i):
                e = probs[:, i, 0:P].rearrange("t (q k) -> t q k", q=2)
                dve.wait_ge(exps, 18 * g + (17 + i))
                dve.reduce_sum(sums3[:, i, :], e, AX_X).then_inc(sums_ready, 1)
                dve.wait_ge(sums_ready, 2 * g + (i + 1))
                dve.reciprocal(recip3[:, i, :], sums3[:, i, :]).then_inc(recip_ready, 1)
                dve.wait_ge(recip_ready, 22 * g + (21 + i))
                for h in range(2):
                    rows = slice(C * h, C * h + C)
                    ins = dve.tensor_tensor(probs3[rows, 2 * i:2 * i + 2, h, :], e[rows],
                                            recip3[rows, i, :].unsqueeze(2).broadcast_to([C, 2, C]), ALU.mult)
                ins.then_inc(probs3_ready, 1)

            def weighted_step(g, step):
                _, l, i = step
                if l == 0:
                    if i % 2 == 0:
                        return
                    n0 = a_at[step]
                    bk, n, released = ring_count(g, n0, a_n)
                    p = i // 2
                    dve.wait_ge(weighted_full[bk], n)
                    sums = weighted[bk][:, 0:4 * V0W].rearrange("t (h u v) -> t h u v", h=2, u=2)
                    rz = recip[:, bk, 0:4].rearrange("t (h u) -> t h u", h=2)
                    dve.reciprocal(rz, sums[:, :, :, C]).then_inc(recip_ready, 1)
                    dve.wait_ge(recip_ready, 22 * g + (p + 1))
                    dve.tensor_tensor(x_scaled[:], sums[:, :, :, 0:C], rz.unsqueeze(3).broadcast_to([P, 2, 2, C]),
                                      ALU.mult).then_inc(weighted_free[bk], 1)
                    dve.wait_ge(weighted_free[bk], released)
                    toks = slice(P * p, P * p + P)
                    dve.tensor_tensor(state[:, :, toks].rearrange("f u (h c) -> f h u c", h=2), x_scaled[:],
                                      xT[:, :, toks].rearrange("f u (h c) -> f h u c", h=2), ALU.add).then_inc(state_sum, 1)
                    if p % 2:
                        dve.wait_ge(state_sum, 4 * g + (p + 1))
                        split_state(g, p // 2, p // 2)
                    return
                if l == 1 and i == 0:
                    dve.wait_ge(result_free, g + 1)
                for c in range(2):
                    n0 = a_at[step] + c
                    bk, n, _ = ring_count(g, n0, a_n)
                    dve.wait_ge(weighted_full[bk], n)
                    sums = weighted[bk][:, 0:4 * 2 * VW].rearrange("t (j h v) -> t j h v", j=4, h=2)
                    rz = recip[:, bk, :].rearrange("t (j h) -> t j h", j=4)
                    dve.reciprocal(rz, sums[:, :, :, VW - 1]).then_inc(recip_ready, 1)
                    dve.wait_ge(recip_ready, 22 * g + (4 + 8 * (l - 1) + 2 * i + c + 1))
                    for q in range(2):
                        rows = slice(C * q, C * q + C)
                        ins = dve.tensor_tensor(attn[rows, i, :, 4 * c:4 * c + 4, :].rearrange("t h j d -> t j h d"),
                                                sums[rows, :, :, HD * q:HD * q + HD],
                                                rz[rows].unsqueeze(3).broadcast_to([C, 4, 2, HD]), ALU.mult)
                    ins.then_inc(weighted_free[bk], 1)

            def stats_step(g, p):
                if p == 0:
                    dve.wait_ge(group_loaded, 48 if g is None else 48 * g + 96)
                for t, src in ((p, x_raw), (NP + p, c_raw)):
                    ins = dve.bn_stats(stats[:, t, :], src[:, p, :])
                ins.then_inc(stats_ready, 1)

            def moments_step(g):
                dve.wait_ge(stats_ready, NP if g is None else NP * g + 2 * NP)
                dve.sem_inc(dve_held, 1)
                for t in range(2 * NP):
                    ins = dve.bn_aggr(mean_var[:, t, :], stats[:, t, :])
                ins.then_inc(mv_ready, 1)

            def sum_columns(g):
                for dst in v2:
                    for h in range(2):
                        rows = slice(C * h, C * h + C)
                        ins = dve.tensor_copy(dst[rows, :, :, h, VW - 1],
                                              mask_col[rows, bass.ds(NP * g, NP)].unsqueeze(2).broadcast_to([C, NP, NJ]))
                ins.then_inc(sum_columns_ready, 1)

            def weight_step(step):
                name = step[1]
                if name in ("Wo3T", "VB1", "VB2"):
                    return
                o, free, n = full(None, step, False)
                if name == "W0T":
                    dve.tensor_copy(mask_col[:], o[:, 3 * P:3 * P + B // 2])
                    dve.tensor_copy(w0T[:], o[:, 0:3 * P].rearrange("a (i b) -> a i b", i=3)).then_inc(free, 1)
                elif name == "W0":
                    dve.tensor_tensor(v0_bias[:], o[:, 0:P].rearrange("k (h c) -> k h c", h=2),
                                      bo_row.unsqueeze(1).broadcast_to([P, 2, C]), ALU.add)
                    dve.tensor_copy(wv0[:], o[:, P:2 * P]).then_inc(free, 1)
                elif name == "MS":
                    dve.tensor_scalar(mask_sum[:], o[:, 0:B // 2], 0.5, None, ALU.max).then_inc(free, 1)
                    dve.wait_ge(free, n)
                    dve.reciprocal(mix_col[:], mask_sum[:]).then_inc(mask_sum_ready, 1)
                    dve.wait_ge(mask_sum_ready, 1)
                    dve.tensor_tensor(mix_col[:], mix_col[:], mask_col[:], ALU.mult).then_inc(mix_col_ready, 1)
                    dve.wait_ge(mix_col_ready, 1)
                else:
                    v = o[:].rearrange("h (k m) -> h k m", k=NK)
                    key = {"M3": "k3", "VW3": "v3"}.get(name, name[1:])
                    hi, lo = wT[key]
                    dve.wait_ge(w_hi, SPLIT_WEIGHTS.index(step) + 1)
                    for k in range(NK):
                        if name[1] in "kv":
                            scalar = gamma[:, int(name[2]) - 1, k:k + 1]
                        else:
                            scalar = D ** -0.5 if name == "M3" else tgates[:, int(name[2]) - 1:int(name[2])] if name[1] == "o" else 1.0
                        ins = dve.scalar_tensor_tensor(out=lo[:, k, :], in0=v[:, k, :], scalar=scalar, in1=hi[:, k, :].bitcast(F32),
                                                       op0=ALU.mult, op1=ALU.subtract)
                    ins.then_inc(free, 1)

            def iteration(g, last):
                for step in (LAST_ORDER if last else ORDER):
                    if step[0] == "E" or step[0] == "P" and ("E",) + step[1:] not in ORDER:
                        proj_step(g, ("P",) + step[1:], last)
                    elif step[0] == "S":
                        scores_step(g, step)
                    elif step[0] == "X" and step[1] == 3:
                        normalise3(g, step[2])
                    elif step[0] == "A":
                        weighted_step(g, step)
                    elif step[0] == "ST":
                        stats_step(g, step[1])
                    elif step[0] == "MV":
                        moments_step(g)
                    elif step[0] == "SC":
                        sum_columns(g)

            def normalise_rows(part):
                dve.wait_ge(rstd_ready if part == 0 else mix_ready, 1)
                src, dst = ((x_raw, x_norm), (c_raw, c_norm))[part]
                for n in range(NP):
                    t = NP * part + n
                    ins = dve.tensor_scalar(dst[:, n, :], src[:, n, :], mean_var[:, t, 0:1], rstd[:, t:t + 1],
                                            ALU.subtract, ALU.mult)
                if part:
                    ins.then_inc(normed, 1)

            dve.memset(w0_bd, 0.0).then_inc(w0_ready, 1)
            for t in (v2[0], v2[1], probs3):
                dve.memset(t[:], 0.0)
            dve.memset(v0[:, :, :, C], 1.0).then_inc(cleared, 1)
            dve.wait_ge(mask_loaded, 16)
            dve.tensor_copy(mask_f[:], mask_u8[:]).then_inc(mask_ready, 1)
            dve.wait_ge(w0_loaded, 4 * 16)
            dve.wait_ge(w0_ready, 1)
            for h in range(2):
                blk_h = slice(C * h, C * h + C)
                ins = dve.tensor_copy(w0_bd[blk_h, :, blk_h], w0_raw[blk_h])
            ins.then_inc(w0_ready, 1)
            for step in PROLOGUE:
                if step in FRONT:
                    proj_step(None, step, False)
                elif step[0] == "P":
                    weight_step(step)
                elif step[0] == "ST":
                    stats_step(None, step[1])
                elif step[0] == "MV":
                    moments_step(None)
                elif step[0] == "TG":
                    dve.wait_ge(b0_loaded, 64)
                    dve.tensor_copy(bl_wide, w0_cols[:, 2:3].broadcast_to([P, P])).then_inc(bl_ready, 1)
                elif step[0] == "NM":
                    normalise_rows(step[1])
            with dve.Fori(0, NG - 1) as g:
                iteration(g, False)
            iteration(NG - 1, True)

        @blk.gpsimd
        def _(pool):
            def hold(signal, n):
                pool.wait_ge(signal, n)
                pool.sem_inc(pool_held, 1)

            def spread_keys(g, l, last):
                for i in range(NK):
                    bk, n = p_count(g, ("P", f"K{l}", i), last)
                    pool.wait_ge(proj_free[bk], n)
                    each = [P, GB, 4, C]
                    pool.tensor_tensor(kbd[l - 1][:, i], k_tmp[:, i, :].rearrange("p (b s) -> p b s", s=C).unsqueeze(2).broadcast_to(each),
                                       own_slot.unsqueeze(1).unsqueeze(3).broadcast_to(each), ALU.mult).then_inc(k_spread, 1)

            def deviations(nth):
                hold(mv_ready, nth)
                pool.tensor_scalar(var_eps[:], mean_var[:, :, 1], EPS, None, ALU.add).then_inc(ve_ready, 1)
                pool.wait_ge(ve_ready, nth)
                pool.tensor_tensor(rstd[:], var_eps[:], half_neg[:], ALU.pow).then_inc(rstd_ready, 1)

            def front(g):
                nth = 1 if g is None else g + 2
                hold(group_loaded, 48 * nth)
                pairs = slice(0, NP) if g is None else bass.ds(NP * g + NP, NP)
                each = [P, NP, P]
                if g is None:
                    w0T_bank, n = p_count(None, ("P", "W0T", 0), False)
                    hold(proj_free[w0T_bank], n)
                pool.tensor_scalar(drop_row, mrow_u8[:], -1.0, 1.0, ALU.mult, ALU.add).then_inc(mix_step, 1)
                pool.tensor_tensor(mix[:], ident.unsqueeze(1).broadcast_to(each),
                                   mask_col[:, pairs].unsqueeze(2).broadcast_to(each), ALU.mult).then_inc(mix_step, 1)
                if g is None:
                    deviations(nth)
                if g is None:
                    hold(mix_col_ready, 1)
                hold(mix_step, 4 * nth - 2)
                pool.tensor_tensor(drop_row, drop_row, mix_col[:, pairs].unsqueeze(2).broadcast_to(each),
                                   ALU.mult).then_inc(mix_step, 1)
                pool.wait_ge(mix_step, 4 * nth - 1)
                pool.tensor_tensor(drop_row, drop_row, block.unsqueeze(1).broadcast_to(each),
                                   ALU.mult).then_inc(mix_step, 1)
                pool.wait_ge(mix_step, 4 * nth)
                pool.tensor_tensor(mix[:], drop_row, mix[:], ALU.add).then_inc(mix_ready, 1)
                if g is None:
                    return
                deviations(nth)
                hold(rstd_ready, nth)
                for t in list(range(NP, 2 * NP)) + list(range(NP)):
                    src, dst = (x_raw, x_norm) if t < NP else (c_raw, c_norm)
                    ins = pool.tensor_scalar(dst[:, t % NP, :], src[:, t % NP, :], mean_var[:, t, 0:1], rstd[:, t:t + 1],
                                             ALU.subtract, ALU.mult)
                ins.then_inc(normed, 1)

            for l in (1, 2):
                for k in range(NK):
                    pool.dma_start(gamma[:, l - 1, k:k + 1],
                                   w[f"L{l}_xattn_ln_gamma"][P * k:P * k + P].unsqueeze(1)).then_inc(scales_loaded, 16)
                pool.dma_start(beta_row[:, l - 1, :],
                               w[f"L{l}_xattn_ln_beta"].unsqueeze(0).broadcast_to([P, D])).then_inc(scales_loaded, 16)
                pool.dma_start(gates[:, l - 1:l],
                               w[f"L{l}_xattn_gate"].unsqueeze(0).broadcast_to([P, 1])).then_inc(scales_loaded, 16)
            pool.dma_start(gates[:, 2:3], w["L3_xattn_alpha"].unsqueeze(0).broadcast_to([P, 1])).then_inc(scales_loaded, 16)
            pool.memset(half_neg[:], -0.5).then_inc(half_ready, 1)
            pool.wait_ge(half_ready, 1)
            front(None)
            pool.wait_ge(scales_loaded, 9 * 16)
            for l, loaded in ((1, w1_loaded), (2, w2_loaded)):
                hold(loaded, 64)
                for m in range(NK):
                    ins = pool.tensor_copy(o_sorted[l - 1][:, m, :].rearrange("o (q j d) -> o q j d", q=2, d=HD),
                                           raw[f"o{l}"][:, m, :].rearrange("o (j q d) -> o q j d", q=2, d=HD))
                ins.then_inc(o_sorted_ready, 1)
                for n, name in enumerate("kv"):
                    pool.tensor_tensor(kv_product[:, 2 * l - 2 + n], raw[f"{name}{l}"][:],
                                       beta_row[:, l - 1, :].unsqueeze(1).broadcast_to([P, NK, D]), ALU.mult).then_inc(kv_ready, 1)
            for l in (1, 2):
                bk, n = p_count(None, ("P", f"VB{l}", 0), False)
                pool.wait_ge(proj_free[bk], n)
                pool.tensor_tensor(kv_product[:, 2 * l - 1], raw[f"o{l}"][:], v_bias_row[l - 1].unsqueeze(1).broadcast_to([P, NK, D]),
                                   ALU.mult).then_inc(o_product_ready, 1)
            pool.sem_inc(k_spread, 2)
            with pool.Fori(0, NG - 1) as g:
                spread_keys(g, 1, False)
                front(g)
                spread_keys(g, 2, False)
            for l in (1, 2):
                spread_keys(NG - 1, l, True)


_WEIGHTS = ['L0_xattn_Wn', 'L0_xattn_bn', 'L0_xattn_Wm', 'L0_xattn_bm', 'L0_xattn_Wl', 'L0_xattn_bl', 'L0_xattn_Wo',
            'L0_xattn_bo', 'L1_xattn_Wq', 'L1_xattn_Wk', 'L1_xattn_Wv', 'L1_xattn_Wo', 'L1_xattn_ln_gamma',
            'L1_xattn_ln_beta', 'L1_xattn_gate', 'L2_xattn_Wq', 'L2_xattn_Wk', 'L2_xattn_Wv', 'L2_xattn_Wo',
            'L2_xattn_ln_gamma', 'L2_xattn_ln_beta', 'L2_xattn_gate', 'L3_xattn_w_q', 'L3_xattn_w_k', 'L3_xattn_w_v',
            'L3_xattn_w_o', 'L3_xattn_alpha']


def kernel(**inputs):
    import numpy as _np
    import concourse.bacc as _bacc
    from concourse import mybir as _mybir
    from concourse.bass_utils import run_bass_kernel_spmd as _run

    nc = _bacc.Bacc("TRN2", target_bir_lowering=False, num_devices=1)
    arrays = {}

    def dram(name, a):
        a = _np.ascontiguousarray(a)
        arrays[f"in_{name}_dram"] = a
        return nc.dram_tensor(f"in_{name}_dram", a.shape, _mybir.dt.from_np(a.dtype), kind="ExternalInput").ap()

    x = dram("x", inputs["x"])
    ctx = dram("ctx_2048", inputs["ctx_2048"])
    mask = dram("mask", _np.asarray(inputs["mask_BxS2_bf1"]).view(_np.uint8))
    w = {n: dram(n, _np.asarray(inputs[n]).reshape(1) if _np.ndim(inputs[n]) == 0 else inputs[n]) for n in _WEIGHTS}
    rows = _np.arange(P)
    same_batch = rows[:, None] // C == rows[None, :] // C
    head_parity = (rows[:, None] // HD % 2 == _np.arange(2)[None, :]) * HD ** -0.5
    own_slot = rows[:, None] // (2 * HD) == _np.arange(4)[None, :]
    const = dram("const", _np.concatenate([_np.eye(P), same_batch, head_parity, own_slot], axis=1).astype(_np.float32))
    y = nc.dram_tensor("out_0_dram", (B, C, D), F32, kind="ExternalOutput").ap()
    build(nc, x, ctx, mask, w, const, y)
    r = _run(nc, [arrays], core_ids=[0])
    return r.results[0]["out_0_dram"]
```
